# Optimizing a Trainium2 kernel written in Bass

```python
import numpy as np
import jax
import jax.numpy as jnp

def _softmax(x, axis=-1):
    return jax.nn.softmax(x, axis=axis)

def _gelu(x):
    return jax.nn.gelu(x, approximate=True)

def _silu(x):
    return jax.nn.silu(x)

def _sigmoid(x):
    return jax.nn.sigmoid(x)

def _layernorm(x, axis=-1, eps=1e-05):
    m = jnp.mean(x, axis=axis, keepdims=True)
    v = jnp.var(x, axis=axis, keepdims=True)
    return (x - m) / jnp.sqrt(v + eps)

def _scatter_add(tgt, idx, src, axis=0):
    return tgt.at[idx].add(src)

def _segment_sum(src, seg, n):
    return jax.ops.segment_sum(src, seg, n)
kernel_name = 'mk_adaln_d1_jaxref_r8_ba6dca'

def setup_inputs(seed: int=0):
    np.random.seed(seed)
    _w = jnp.asarray

    def _L0_attn_setup():
        import jax, jax.numpy as jnp
        import numpy as np
        DIM = 256
        HIDDEN = 256
        HEADS = 4
        HD = HIDDEN // HEADS
        EPS = 1e-06
        BATCH = 4
        SEQ = 256
        key = jax.random.key(seed)
        k0, k1, k2, k3 = jax.random.split(key, 4)
        s = 0.02
        x = jax.random.normal(k0, (BATCH, SEQ, DIM), dtype=jnp.float32)
        W_in = jax.random.normal(k1, (HIDDEN, DIM), dtype=jnp.float32) * s
        W_gate = jax.random.normal(k2, (4 * HIDDEN, HIDDEN), dtype=jnp.float32) * s
        b_gate = jnp.zeros((4 * HIDDEN,), dtype=jnp.float32)
        rms_w = jnp.ones((HD,), dtype=jnp.float32)
        W_out = jax.random.normal(k3, (DIM, HIDDEN), dtype=jnp.float32) * s
        return {'x': x, 'W_in': W_in, 'W_gate': W_gate, 'b_gate': b_gate, 'rms_w': rms_w, 'W_out': W_out}
    _L0_attn_in = _L0_attn_setup()

    def _L0_ffn_setup():
        import jax, jax.numpy as jnp
        import numpy as np
        H, I, E, TOP_K = (256, 176, 16, 6)
        IS = 352
        NORM_TOPK_PROB = False

        def _silu_and_mul(gate_up):
            d = gate_up.shape[-1] // 2
            g, u = (gate_up[..., :d], gate_up[..., d:])
            return jax.nn.silu(g) * u
        key = jax.random.key(seed)
        ks = jax.random.split(key, 6)
        s = 0.02
        return {'x': jax.random.normal(ks[0], (1, 256, H), jnp.float32), 'gate_w': jax.random.normal(ks[1], (E, H), jnp.float32) * s, 'w1': jax.random.normal(ks[2], (E, 2 * I, H), jnp.float32) * s, 'w2': jax.random.normal(ks[3], (E, H, I), jnp.float32) * s, 'shared_w1': jax.random.normal(ks[4], (2 * IS, H), jnp.float32) * s, 'shared_w2': jax.random.normal(ks[5], (H, IS), jnp.float32) * s}
    _L0_ffn_in = _L0_ffn_setup()
    _L0_c = _w((lambda *s: np.random.randn(*s).astype(np.float32) * 0.05)(4, 256))
    _L0_wmod = _w((lambda *s: np.random.randn(*s).astype(np.float32) * 0.05)(256, 6 * 256) * 256 ** (-0.5))
    _d = {'L0_attn_x': _L0_attn_in['x'], 'L0_attn_W_in': _L0_attn_in['W_in'], 'L0_attn_W_gate': _L0_attn_in['W_gate'], 'L0_attn_b_gate': _L0_attn_in['b_gate'], 'L0_attn_rms_w': _L0_attn_in['rms_w'], 'L0_attn_W_out': _L0_attn_in['W_out'], 'L0_ffn_gate_w': _L0_ffn_in['gate_w'], 'L0_ffn_w1': _L0_ffn_in['w1'], 'L0_ffn_w2': _L0_ffn_in['w2'], 'L0_ffn_shared_w1': _L0_ffn_in['shared_w1'], 'L0_ffn_shared_w2': _L0_ffn_in['shared_w2'], 'L0_c': _L0_c, 'L0_wmod': _L0_wmod}
    _x0 = _d['L0_attn_x']
    _d['L0_attn_x'] = jax.random.normal(jax.random.fold_in(jax.random.key(seed), 1), (4, 512, 256), dtype=_x0.dtype)
    del _x0
    return _d

def reference(L0_attn_x, L0_attn_W_in, L0_attn_W_gate, L0_attn_b_gate, L0_attn_rms_w, L0_attn_W_out, L0_ffn_gate_w, L0_ffn_w1, L0_ffn_w2, L0_ffn_shared_w1, L0_ffn_shared_w2, L0_c, L0_wmod):

    def _L0_attn_ref(x, W_in, W_gate, b_gate, rms_w, W_out):
        import jax, jax.numpy as jnp
        import numpy as np
        DIM = 256
        HIDDEN = 256
        HEADS = 4
        HD = HIDDEN // HEADS
        EPS = 1e-06
        BATCH = 4
        SEQ = 256
        B, L, _ = x.shape
        xp = x @ W_in.T
        gates = xp @ W_gate.T + b_gate
        gates = gates.reshape(B, L, HEADS, 4 * HD).transpose(0, 2, 1, 3)
        i_g, f_g, o_g, c_t = jnp.split(gates, 4, axis=-1)
        i_g = jnp.exp(i_g)
        f_g = jax.nn.sigmoid(f_g)
        o_g = jax.nn.sigmoid(o_g)
        c_t = jnp.tanh(c_t)
        tm = lambda a: jnp.moveaxis(a, 2, 0)

        def step(c, g):
            i, f, o, cd = g
            c = f * c + i * cd
            c_norm = c * jax.lax.rsqrt(jnp.mean(c * c, axis=-1, keepdims=True) + EPS) * rms_w
            h = o * jnp.tanh(c_norm)
            return (c, h)
        c0 = jnp.zeros((B, HEADS, HD), dtype=x.dtype)
        _, hs = jax.lax.scan(step, c0, (tm(i_g), tm(f_g), tm(o_g), tm(c_t)))
        h_out = jnp.moveaxis(hs, 0, 1).reshape(B, L, HIDDEN)
        return h_out @ W_out.T

    def _L0_ffn_ref(x, gate_w, w1, w2, shared_w1, shared_w2):
        import jax, jax.numpy as jnp
        import numpy as np
        H, I, E, TOP_K = (256, 176, 16, 6)
        IS = 352
        NORM_TOPK_PROB = False

        def _silu_and_mul(gate_up):
            d = gate_up.shape[-1] // 2
            g, u = (gate_up[..., :d], gate_up[..., d:])
            return jax.nn.silu(g) * u
        B, S, Hd = x.shape
        xf = x.reshape(-1, Hd)
        T = xf.shape[0]
        shared_out = _silu_and_mul(xf @ shared_w1.T) @ shared_w2.T
        logits = xf @ gate_w.T
        probs = jax.nn.softmax(logits.astype(jnp.float32), axis=-1)
        routing_weights, selected = jax.lax.top_k(probs, TOP_K)
        if NORM_TOPK_PROB:
            routing_weights = routing_weights / routing_weights.sum(-1, keepdims=True)
        combine = jnp.zeros((T, E), jnp.float32).at[jnp.arange(T)[:, None], selected].add(routing_weights).astype(x.dtype)
        gate_up = jnp.einsum('th,eoh->teo', xf, w1)
        act = _silu_and_mul(gate_up)
        moe_out = jnp.einsum('te,tei,ehi->th', combine, act, w2)
        return (moe_out + shared_out).reshape(B, S, Hd)
    x = L0_attn_x
    mod = (_silu(L0_c) @ L0_wmod).reshape(L0_c.shape[0], 6, 1, -1)
    sa, ca, ga, sb, cb, gb = (mod[:, 0], mod[:, 1], mod[:, 2], mod[:, 3], mod[:, 4], mod[:, 5])
    ga = (2 * (ga >= 0) - 1) * jnp.maximum(jnp.abs(ga), 0.25)
    gb = (2 * (gb >= 0) - 1) * jnp.maximum(jnp.abs(gb), 0.25)
    h = _layernorm(x, axis=-1) * (1 + ca) + sa
    x = x + ga * _L0_attn_ref(h, L0_attn_W_in, L0_attn_W_gate, L0_attn_b_gate, L0_attn_rms_w, L0_attn_W_out)
    h = _layernorm(x, axis=-1) * (1 + cb) + sb
    x = x + gb * _L0_ffn_ref(h, L0_ffn_gate_w, L0_ffn_w1, L0_ffn_w2, L0_ffn_shared_w1, L0_ffn_shared_w2)
    return x

_drawn_inputs = setup_inputs


def setup_inputs(seed=0):
    import zlib

    import numpy as np

    out = dict(_drawn_inputs(seed))
    spreads = {'L0_attn_b_gate': (0.0, 0.321), 'L0_attn_rms_w': (1.0, 0.6)}
    factors = {'L0_attn_W_in': 4.051,
     'L0_attn_W_gate': 3.961,
     'L0_ffn_gate_w': 8.0,
     'L0_ffn_w1': 8.0,
     'L0_ffn_w2': 8.0,
     'L0_ffn_shared_w1': 8.0,
     'L0_ffn_shared_w2': 8.0}
    for name, (base, spread) in spreads.items():
        noise = np.random.default_rng([zlib.crc32(name.encode()), seed]).standard_normal(out[name].shape)
        drawn = base * np.exp(spread * noise) if base else spread * noise
        out[name] = jnp.asarray(drawn.astype(out[name].dtype))
    for name, factor in factors.items():
        out[name] = (out[name] * factor).astype(out[name].dtype)
    return out
```

```python
from contextlib import ExitStack

import numpy as np

import concourse.bass as bass
from concourse import mybir

F32 = mybir.dt.float32
F32R = mybir.dt.float32r
I32 = mybir.dt.int32
ALU = mybir.AluOpType
ACT = mybir.ActivationFunctionType
AX = mybir.AxisListType

P = 128
BATCH, SEQ, DIM = 4, 512, 256
HEADS, HEAD_DIM = 4, 64
EXPERTS, EXPERT_HIDDEN, TOP_K = 16, 176, 6
SHARED_HIDDEN = 352
LN_EPS, RMS_EPS, GATE_FLOOR = 1e-5, 1e-6, 0.25

KT = DIM // P
TT = SEQ // P
GATE_I, GATE_F, GATE_O, GATE_C = range(4)
HEADS_PER_TILE = P // HEAD_DIM
SHARED_SLOTS = -(-SHARED_HIDDEN // P)
ROUTED_SLOTS = EXPERTS * EXPERT_HIDDEN // P
SLOTS = SHARED_SLOTS + ROUTED_SLOTS
UP_COLS = KT * 2 * P
SLOT_COLS = UP_COLS + DIM
SHIFT_A, SCALE_A, GAIN_A, SHIFT_B, SCALE_B, GAIN_B = range(6)
MODS = 6
MAX8 = 8
BIG_PROB = 2.0
RSQRT_SEED = float(0x5F3759DF)
DOWN_LAG = 2
ROUTING_RING = 4
DOWN_RING = 4
PREPARE_FROM_SLOT = 5


class Engine:

    def __init__(self, counts):
        self.steps, self.counts, self.waited = [], counts, {}

    def wait(self, *marks):
        for sem, value in marks:
            if self.waited.get(id(sem), 0) < value:
                self.waited[id(sem)] = value
                self.steps.append(lambda e, s=sem, v=value: e.wait_ge(s, v))

    def do(self, step, sem=None, by=1):
        if sem is None:
            self.steps.append(step)
            return None
        self.counts[id(sem)] = self.counts.get(id(sem), 0) + by
        self.steps.append(lambda e: step(e).then_inc(sem, by))
        return (sem, self.counts[id(sem)])

    def play(self, e):
        for step in self.steps:
            step(e)


def adaln_program(nc, x_in, w_in, w_gate_t, b_gate, rms_w, w_out_t, router_t, shared_w, routed_w,
                  cond_t, w_mod, out):
    ctx = ExitStack()
    with ctx:
        def sb(name, shape, dt=F32):
            return ctx.enter_context(nc.sbuf_tensor(name, shape, dt))

        def sem(name):
            return ctx.enter_context(nc.semaphore(name))

        routing_dram = nc.dram_tensor("routing_dram", [BATCH, EXPERTS, SEQ], F32, kind="Internal").ap()

        ident = sb("ident", [P, P])
        head_mean = sb("head_mean", [P, HEADS_PER_TILE])
        w_slots = sb("w_slots", [P, SLOTS, SLOT_COLS])
        w_gates_hi = sb("w_gates_hi", [P, KT, 4 * DIM], F32R)
        w_gates_lo = sb("w_gates_lo", [P, KT, 4 * DIM], F32R)
        w_out_hi = sb("w_out_hi", [P, KT, DIM], F32R)
        w_out_lo = sb("w_out_lo", [P, KT, DIM], F32R)
        router_w = sb("router_w", [P, KT, EXPERTS])
        gate_bias = sb("gate_bias", [P, 4 * KT])
        half_bias = sb("half_bias", [P, 4 * KT])
        rms_scale = sb("rms_scale", [P, 1])
        cond = sb("cond", [P, KT, BATCH])
        cond_tanh = sb("cond_tanh", [P, KT, BATCH])
        cond_silu = sb("cond_silu", [P, KT, BATCH])
        mod = sb("mod", [P, MODS, KT, BATCH])
        gain_sign = sb("gain_sign", [P, KT, BATCH])
        gain_abs = sb("gain_abs", [P, KT, BATCH])

        x_rows = [sb(f"x_rows{i}", [P, TT, DIM]) for i in range(2)]
        h_hi = [sb(f"h_hi{i}", [P, KT, SEQ], F32R) for i in range(2)]
        h_lo = [sb(f"h_lo{i}", [P, KT, SEQ], F32R) for i in range(2)]
        work = sb("work", [P, 5, KT, SEQ])
        gate_i, gate_c, gate_f, gate_o, cell = (work[:, n] for n in range(5))
        mixed = sb("mixed", [P, KT, SEQ])
        cell_out_hi = sb("cell_out_hi", [P, KT, SEQ], F32R)
        cell_out_lo = sb("cell_out_lo", [P, KT, SEQ], F32R)
        h_full = gate_i
        normed = work[:, 1].rearrange("p k t -> p (k t)").rearrange("p (t d) -> p t d", d=DIM)
        square, cell_tanh = gate_c, gate_c
        inv_rms_wide = work[:, 2].rearrange("p k t -> p (k t)").rearrange("p (k t c) -> p k t c", k=KT, c=P)
        cell_out = gate_i
        projected = cell
        w_mod_raw = work[:, 0:3].rearrange("p n k t -> p (n k t)").rearrange("p (k m) -> p k m", k=KT)
        w_gate_raw = work[:, 3:5].rearrange("p n k t -> p (n k t)").rearrange("p (k m) -> p k m", k=KT)
        mixed_flat = mixed[:, :, :].rearrange("p k t -> p (k t)")
        w_in_raw = mixed_flat[:, 0:KT * DIM].rearrange("p (k m) -> p k m", k=KT)
        w_out_raw = mixed_flat[:, KT * DIM:2 * KT * DIM].rearrange("p (k m) -> p k m", k=KT)

        stats = sb("stats", [P, TT, 6])
        mean_var = sb("mean_var", [P, TT, 2])
        ln_in = sb("ln_in", [P, TT])
        ln_seed = sb("ln_seed", [P, TT], I32)
        ln_y = sb("ln_y", [P, TT], I32)
        ln_t = sb("ln_t", [P, TT])
        NORMS = KT * TT * HEADS_PER_TILE
        rms_in = sb("rms_in", [P, NORMS])
        rms_seed = sb("rms_seed", [P, NORMS], I32)
        rms_y = sb("rms_y", [P, NORMS], I32)
        rms_t = sb("rms_t", [P, NORMS])
        neg_max = sb("neg_max", [P, TT])
        shifted = sb("shifted", [P, TT, EXPERTS])
        exps = sb("exps", [P, TT, EXPERTS])
        exp_sum = sb("exp_sum", [P, TT])
        exp_inv = sb("exp_inv", [P, TT])
        PADDED = EXPERTS + MAX8 - TOP_K
        probs = sb("probs", [P, TT, PADDED])
        best8 = sb("best8", [P, TT, MAX8])
        taken = sb("taken", [P, TT, PADDED])
        routing = sb("routing", [P, TT, EXPERTS])
        routing_t = sb("routing_t", [EXPERTS, SEQ])

        up_hi = [sb(f"up_hi{i}", [P, UP_COLS], F32R) for i in range(2)]
        up_lo = [sb(f"up_lo{i}", [P, UP_COLS], F32R) for i in range(2)]
        down_hi = [sb(f"down_hi{i}", [P, DIM], F32R) for i in range(DOWN_RING)]
        down_lo = [sb(f"down_lo{i}", [P, DIM], F32R) for i in range(DOWN_RING)]
        hidden = [sb(f"hidden{i}", [P, SEQ]) for i in range(3)]
        act_hi = [sb(f"act_hi{i}", [P, SEQ], F32R) for i in range(2)]
        act_lo = [sb(f"act_lo{i}", [P, SEQ], F32R) for i in range(2)]
        routing_rows = [sb(f"routing_rows{i}", [P, SEQ]) for i in range(ROUTING_RING)]

        def bank(name):
            return ctx.enter_context(nc.psum_tensor(name, [P, SEQ], F32))

        pre = [bank(f"pre{i}") for i in range(2)]
        gate_ps = [bank(f"gate_ps{i}") for i in range(2)]
        up_ps = [bank(f"up_ps{i}") for i in range(2)]
        sum_ps = [bank(f"sum_ps{i}") for i in range(KT)]

        counts = {}
        sp, pe, act, dve, pool = (Engine(counts) for _ in range(5))

        s_load = {n: sem(f"s_load_{n}") for n in
                  ("w_mod", "cond", "w_gate", "w_in", "w_out", "small", "router")}
        s_x = [sem(f"s_x{i}") for i in range(2)]
        W_PARTS = [(0, 1), (1, 3), (3, 8), (8, 14), (14, 20), (20, SLOTS)]
        s_w = [sem(f"s_w{i}") for i in range(len(W_PARTS))]
        s_store = [sem(f"s_store{i}") for i in range(2)]
        s_routing_dram = sem("s_routing_dram")
        s_rows = [sem(f"s_rows{i}") for i in range(ROUTING_RING)]
        s_const, s_setup_act, s_setup_dve, s_setup_pe = (sem(n) for n in (
            "s_const", "s_setup_act", "s_setup_dve", "s_setup_pe"))
        s_prep_pe, s_prep_act, s_prep_dve, s_prep_pool = (sem(n) for n in (
            "s_prep_pe", "s_prep_act", "s_prep_dve", "s_prep_pool"))
        s_fin_pe, s_fin_act, s_fin_dve = (sem(n) for n in ("s_fin_pe", "s_fin_act", "s_fin_dve"))
        s_gate_mm, s_up_mm, s_down_mm = (sem(n) for n in ("s_gate_mm", "s_up_mm", "s_down_mm"))
        s_split_hi, s_split_lo = sem("s_split_hi"), sem("s_split_lo")
        s_tanh, s_silu, s_routed, s_act, s_act_hi, s_act_lo = (sem(n) for n in (
            "s_tanh", "s_silu", "s_routed", "s_act", "s_act_hi", "s_act_lo"))

        def split_products(dst, pairs, sem_=None):
            last, n = None, 0
            for (a_hi, a_lo), (b_hi, b_lo) in pairs:
                for a, b in ((a_hi, b_hi), (a_hi, b_lo), (a_lo, b_hi)):
                    n += 1
                    first, end = n == 1, n == 3 * len(pairs)
                    last = pe.do(lambda e, a=a, b=b, f=first, l=end: e.matmul(dst, a, b, start=f, stop=l),
                                 sem_ if end else None)
            return last

        def load(queue, dst, src, sem_):
            return queue.do(lambda e: e.dma_start(dst, src), sem_, 16)

        x_in_rows = x_in.rearrange("b (t p) d -> b p t d", p=P)
        out_rows = out.rearrange("b (t p) d -> b p t d", p=P)
        x_loaded = {0: load(sp, x_rows[0][:, :, :], x_in_rows[0], s_x[0])}
        load(sp, cond[:, :, :], cond_t.rearrange("(k p) b -> p k b", p=P), s_load["cond"])
        cond_in = (s_load["cond"], 16)
        w_in_in = load(sp, w_in_raw, w_in.rearrange("(k p) m -> p k m", p=P), s_load["w_in"])
        w_gate_in = load(sp, w_gate_raw, w_gate_t.rearrange("(k p) m -> p k m", p=P), s_load["w_gate"])
        w_mod_in = load(act, w_mod_raw, w_mod.rearrange("(k p) m -> p k m", p=P), s_load["w_mod"])
        load(sp, gate_bias[:, :], b_gate, s_load["small"])
        for h in range(HEADS_PER_TILE):
            small_in = load(sp, rms_scale[h * HEAD_DIM:(h + 1) * HEAD_DIM, :], rms_w, s_load["small"])
        w_out_in = load(sp, w_out_raw, w_out_t.rearrange("(k p) m -> p k m", p=P), s_load["w_out"])
        router_in = load(sp, router_w[:, :, :], router_t.rearrange("(k p) m -> p k m", p=P), s_load["router"])
        w_loaded = {}
        for i, (a, b) in enumerate(W_PARTS):
            src = shared_w[:, a:b, :] if b <= SHARED_SLOTS else routed_w[:, a - SHARED_SLOTS:b - SHARED_SLOTS, :]
            mark = load(sp, w_slots[:, a:b, :], src, s_w[i])
            for s in range(a, b):
                w_loaded[s] = mark
        x_loaded[1] = load(sp, x_rows[1][:, :, :], x_in_rows[1], s_x[1])

        pool.do(lambda e: e.memset(ident[:, :], 0.0), s_const)
        pool.do(lambda e: e.memset(head_mean[:, :], 0.0), s_const)
        zeroed = pool.do(lambda e: e.memset(probs[:, :, EXPERTS:PADDED], BIG_PROB), s_const)
        pool.wait(zeroed)
        consts_in = pool.do(lambda e: e.affine_select(out=ident[:, :], in_=ident[:, :], compare_op=ALU.not_equal, fill=1.0,
                                          base=0, pattern=[[-1, P]], channel_multiplier=1), s_const)
        for h in range(HEADS_PER_TILE):
            pool.wait(consts_in)
            consts_in = pool.do(lambda e, h=h: e.memset(
                head_mean[h * HEAD_DIM:(h + 1) * HEAD_DIM, h:h + 1], 1.0 / HEAD_DIM), s_const)

        pool.wait(consts_in)
        act.wait(cond_in)
        m = act.do(lambda e: e.activation(cond_tanh[:, :, :], cond[:, :, :], ACT.Tanh, scale=0.5), s_setup_act)
        dve.wait(m)
        silu2 = dve.do(lambda e: e.scalar_tensor_tensor(
            out=cond_silu[:, :, :], in0=cond_tanh[:, :, :], scalar=1.0, in1=cond[:, :, :],
            op0=ALU.add, op1=ALU.mult), s_setup_dve)
        pe.wait(silu2, w_mod_in, consts_in)
        mod_ps = pre[0][:, 0:MODS * KT * BATCH]
        for n in range(MODS * KT):
            for k in range(KT):
                m = pe.do(lambda e, n=n, k=k: e.matmul(
                    mod_ps[:, n * BATCH:(n + 1) * BATCH], w_mod_raw[:, k, n * P:(n + 1) * P], cond_silu[:, k, :],
                    start=k == 0, stop=k == KT - 1), s_setup_pe)
        dve.wait(m)
        mod_done = dve.do(lambda e: e.tensor_scalar(
            mod[:, :, :, :], mod_ps.rearrange("p (m k b) -> p m k b", m=MODS, k=KT), 0.5, None, ALU.mult),
            s_setup_dve)
        dve.wait(mod_done)
        for i in (SCALE_A, SCALE_B):
            dve.do(lambda e, i=i: e.tensor_scalar(mod[:, i], mod[:, i], 1.0, None, ALU.add), s_setup_dve)
        for i in (GAIN_A, GAIN_B):
            m = dve.do(lambda e, i=i: e.tensor_scalar(gain_sign[:, :, :], mod[:, i], 0.0, 2.0,
                                                      ALU.is_ge, ALU.mult), s_setup_dve)
            dve.wait(m)
            m = dve.do(lambda e: e.tensor_scalar(gain_sign[:, :, :], gain_sign[:, :, :], -1.0, None,
                                                 ALU.add), s_setup_dve)
            dve.wait(m)
            m = dve.do(lambda e, i=i: e.tensor_tensor(gain_abs[:, :, :], mod[:, i], gain_sign[:, :, :],
                                                      ALU.mult), s_setup_dve)
            dve.wait(m)
            m = dve.do(lambda e: e.tensor_scalar(gain_abs[:, :, :], gain_abs[:, :, :], GATE_FLOOR, 0.5,
                                                 ALU.max, ALU.mult), s_setup_dve)
            dve.wait(m)
            m = dve.do(lambda e, i=i: e.tensor_tensor(mod[:, i], gain_abs[:, :, :], gain_sign[:, :, :],
                                                      ALU.mult), s_setup_dve)
            dve.wait(m)
        mod_ready = m
        dve.wait((s_load["small"], small_in[1]))
        bias_ready = dve.do(lambda e: e.tensor_scalar(half_bias[:, :], gate_bias[:, :], 0.5, None, ALU.mult),
                            s_setup_dve)

        pe.wait(w_in_in, w_gate_in, mod_done)
        combined = [(k, half) for k in range(KT) for half in range(2)]
        combined_ps = [pre[1], gate_ps[0], gate_ps[1], up_ps[0]]
        for n, (k, half) in enumerate(combined):
            cols = slice(half * SEQ, (half + 1) * SEQ)
            for kk in range(KT):
                m = pe.do(lambda e, n=n, k=k, kk=kk, cols=cols: e.matmul(
                    combined_ps[n][:, :], w_in_raw[:, kk, k * P:(k + 1) * P], w_gate_raw[:, kk, cols],
                    start=kk == 0, stop=kk == KT - 1), s_setup_pe)
            act.wait(m)
            hi = act.do(lambda e, n=n, k=k, cols=cols: e.copy(w_gates_hi[:, k, cols], combined_ps[n][:, :]), s_setup_act)
            dve.wait(hi)
            w_gates_ready = dve.do(lambda e, n=n, k=k, cols=cols: e.tensor_tensor(
                w_gates_lo[:, k, cols], combined_ps[n][:, :], w_gates_hi[:, k, cols].bitcast(F32),
                ALU.subtract), s_setup_dve)
        combined_done = m
        act.wait(w_out_in)
        hi = act.do(lambda e: e.copy(w_out_hi[:, :, :], w_out_raw), s_setup_act)
        pool.wait(hi)
        w_out_ready = pool.do(lambda e: e.tensor_tensor(
            w_out_lo[:, :, :], w_out_raw, w_out_hi[:, :, :].bitcast(F32), ALU.subtract), s_const)
        w_out_split = w_out_ready

        pre_free = [[w_gates_ready], [w_gates_ready]]

        def rsqrt(value, seed, y, tmp, sem_):
            yf = y.bitcast(F32)
            m = dve.do(lambda e: e.tensor_scalar(seed, value.bitcast(I32), 1, None, ALU.logical_shift_right), sem_)
            dve.wait(m)
            m = dve.do(lambda e: e.tensor_scalar(y, seed, -1.0, RSQRT_SEED, ALU.mult, ALU.add), sem_)
            for _ in range(3):
                dve.wait(m)
                m = dve.do(lambda e: e.tensor_tensor(tmp, value, yf, ALU.mult), sem_)
                dve.wait(m)
                m = dve.do(lambda e: e.scalar_tensor_tensor(out=tmp, in0=tmp, scalar=-0.5, in1=yf,
                                                            op0=ALU.mult, op1=ALU.mult), sem_)
                dve.wait(m)
                m = dve.do(lambda e: e.scalar_tensor_tensor(out=yf, in0=tmp, scalar=1.5, in1=yf,
                                                            op0=ALU.add, op1=ALU.mult), sem_)
            dve.wait(m)
            return m

        def norm_rows(rows, ready):
            dve.wait(*ready)
            for t in range(TT):
                m = dve.do(lambda e, t=t: e.bn_stats(stats[:, t, :], rows[:, t, :]), s_prep_dve)
            dve.wait(m)
            for t in range(TT):
                m = dve.do(lambda e, t=t: e.bn_aggr(mean_var[:, t, :], stats[:, t, :]), s_prep_dve)
            dve.wait(m)
            m = dve.do(lambda e: e.tensor_scalar(ln_in[:, :], mean_var[:, :, 1], LN_EPS, None, ALU.add), s_prep_dve)
            dve.wait(m)
            rsqrt(ln_in[:, :], ln_seed[:, :], ln_y[:, :], ln_t[:, :], s_prep_dve)
            inv = ln_y[:, :].bitcast(F32)
            for t in range(TT):
                m = dve.do(lambda e, t=t: e.tensor_scalar(
                    normed[:, t, :], rows[:, t, :], mean_var[:, t, 0:1], inv[:, t:t + 1],
                    ALU.subtract, ALU.mult), s_prep_dve)
            return m

        def turn_and_modulate(b, normed_ready, scale, shift, h, h_free):
            pe.wait(normed_ready)
            for k in range(KT):
                pe.wait(*pre_free[k])
                for t in range(TT):
                    m = pe.do(lambda e, k=k, t=t: e.transpose(
                        pre[k][:, t * P:(t + 1) * P], normed[:, t, k * P:(k + 1) * P], ident[:, :]),
                        s_prep_pe if t == TT - 1 else None)
                dve.wait(m)
                full = dve.do(lambda e, k=k: e.tensor_scalar(
                    h_full[:, k, :], pre[k][:, :], mod[:, scale, k, b:b + 1], mod[:, shift, k, b:b + 1],
                    ALU.mult, ALU.add), s_prep_dve)
                pre_free[k] = [full]
                act.wait(full, *h_free)
                hi = act.do(lambda e, k=k: e.copy(h_hi[h][:, k, :], h_full[:, k, :]), s_prep_act)
                pool.wait(hi)
                lo = pool.do(lambda e, k=k: e.tensor_tensor(
                    h_lo[h][:, k, :], h_full[:, k, :], h_hi[h][:, k, :].bitcast(F32), ALU.subtract), s_prep_pool)
            return full, lo

        block_up_done = {}
        finished = {}
        rows_ready = {}
        h_ready = {}
        routing_ready = {}

        def prepare(b):
            rows, h = x_rows[b % 2], b % 2
            h_free = [block_up_done[b - 2]] if b >= 2 else []
            ready = [x_loaded[b]]
            if b == 0:
                ready += [w_gates_ready, mod_ready]
            m = norm_rows(rows, ready)
            yield
            full, lo = turn_and_modulate(b, m, SCALE_A, SHIFT_A, h, h_free)
            yield
            pe.wait(lo, w_gates_ready)
            n = 0
            scanned, o_ready = {}, {}
            for k in range(KT):
                marks = {}
                for gate, dst, func, scale, bias in (
                        (GATE_C, gate_c, ACT.Tanh, 1.0, gate_bias), (GATE_I, gate_i, ACT.Exp, 1.0, gate_bias),
                        (GATE_F, gate_f, ACT.Tanh, 0.5, half_bias), (GATE_O, gate_o, ACT.Tanh, 0.5, half_bias)):
                    cols = slice((gate * KT + k) * P, (gate * KT + k + 1) * P)
                    col = slice(gate * KT + k, gate * KT + k + 1)
                    p = n % 2
                    n += 1
                    pe.wait(*pre_free[p])
                    mm = split_products(pre[p][:, :], [
                        ((w_gates_hi[:, kk, cols], w_gates_lo[:, kk, cols]),
                         (h_hi[h][:, kk, :], h_lo[h][:, kk, :])) for kk in range(KT)], s_prep_pe)
                    act.wait(mm, bias_ready)
                    marks[gate] = act.do(lambda e, p=p, k=k, dst=dst, func=func, scale=scale, bias=bias, col=col:
                                         e.activation(dst[:, k, :], pre[p][:, :], func, bias=bias[:, col],
                                                      scale=scale), s_prep_act)
                    pre_free[p] = [marks[gate]]
                    if n % 2 == 0:
                        yield
                pool.wait(marks[GATE_I], marks[GATE_C])
                m_i = pool.do(lambda e, k=k: e.tensor_tensor(gate_i[:, k, :], gate_i[:, k, :], gate_c[:, k, :],
                                                             ALU.mult), s_prep_pool)
                dve.wait(marks[GATE_F])
                m_f = dve.do(lambda e, k=k: e.tensor_scalar(gate_f[:, k, :], gate_f[:, k, :], 0.5, 0.5,
                                                            ALU.mult, ALU.add), s_prep_dve)
                dve.wait(m_i, m_f)
                scanned[k] = dve.do(lambda e, k=k: e.tensor_tensor_scan(
                    cell[:, k, :], gate_f[:, k, :], gate_i[:, k, :], 0.0, ALU.mult, ALU.add), s_prep_dve)
                act.wait(scanned[k])
                squared = act.do(lambda e, k=k: e.activation(square[:, k, :], cell[:, k, :], ACT.Square), s_prep_act)
                o_ready[k] = marks[GATE_O]
            gates_done = mm
            yield
            pe.wait(squared, *pre_free[0])
            for k in range(KT):
                for t in range(TT):
                    at = (k * TT + t) * HEADS_PER_TILE
                    m = pe.do(lambda e, k=k, t=t, at=at: e.matmul(
                        pre[0][:, at:at + HEADS_PER_TILE], square[:, k, t * P:(t + 1) * P], head_mean[:, :],
                        start=True, stop=True), s_prep_pe)
            dve.wait(m)
            m = dve.do(lambda e: e.tensor_scalar(rms_in[:, :], pre[0][:, 0:NORMS], RMS_EPS, None, ALU.add), s_prep_dve)
            pre_free[0] = [m]
            dve.wait(m)
            rsqrt(rms_in[:, :], rms_seed[:, :], rms_y[:, :], rms_t[:, :], s_prep_dve)
            inv = rms_y[:, :].bitcast(F32).rearrange("p (n o) -> p n o", o=1)
            wide = inv_rms_wide.rearrange("p k t c -> p (k t c)").rearrange("p (n d) -> p n d", d=HEAD_DIM)
            spread = dve.do(lambda e: e.tensor_copy(wide, inv.broadcast_to([P, NORMS, HEAD_DIM])), s_prep_dve)
            yield
            pe.wait(spread)
            for k in range(KT):
                pe.wait(*pre_free[k])
                for t in range(TT):
                    m = pe.do(lambda e, k=k, t=t: e.transpose(pre[k][:, t * P:(t + 1) * P],
                                                              inv_rms_wide[:, k, t, :], ident[:, :]), s_prep_pe)
                dve.wait(m)
                m = dve.do(lambda e, k=k: e.tensor_tensor(cell[:, k, :], cell[:, k, :], pre[k][:, :], ALU.mult),
                           s_prep_dve)
                pre_free[k] = [m]
                act.wait(m)
                m = act.do(lambda e, k=k: e.activation(cell_tanh[:, k, :], cell[:, k, :], ACT.Tanh,
                                                       scale=rms_scale[:, 0:1]), s_prep_act)
                dve.wait(m, o_ready[k])
                m = dve.do(lambda e, k=k: e.scalar_tensor_tensor(
                    out=cell_out[:, k, :], in0=gate_o[:, k, :], scalar=1.0, in1=cell_tanh[:, k, :],
                    op0=ALU.add, op1=ALU.mult), s_prep_dve)
                act.wait(m)
                hi = act.do(lambda e, k=k: e.copy(cell_out_hi[:, k, :], cell_out[:, k, :]), s_prep_act)
                pool.wait(hi)
                lo = pool.do(lambda e, k=k: e.tensor_tensor(
                    cell_out_lo[:, k, :], cell_out[:, k, :], cell_out_hi[:, k, :].bitcast(F32), ALU.subtract),
                    s_prep_pool)
            yield
            yield
            pe.wait(lo, w_out_ready)
            for k in range(KT):
                pe.wait(*pre_free[k])
                m = split_products(pre[k][:, :], [
                    ((w_out_hi[:, kk, k * P:(k + 1) * P], w_out_lo[:, kk, k * P:(k + 1) * P]),
                     (cell_out_hi[:, kk, :], cell_out_lo[:, kk, :])) for kk in range(KT)], s_prep_pe)
                act.wait(m)
                m = act.do(lambda e, k=k: e.activation(projected[:, k, :], pre[k][:, :], ACT.Copy,
                                                       scale=mod[:, GAIN_A, k, b:b + 1]), s_prep_act)
                pre_free[k] = [m]
            yield
            add_turned(rows, projected, m, s_prep_pe, s_prep_dve)
            rows_ready[b] = m = (s_prep_dve, counts[id(s_prep_dve)])
            m = norm_rows(rows, [m])
            yield
            full, lo = turn_and_modulate(b, m, SCALE_B, SHIFT_B, h, [gates_done])
            h_ready[b] = lo
            yield
            pe.wait(full, router_in, *pre_free[0])
            for t in range(TT):
                for k in range(KT):
                    m = pe.do(lambda e, t=t, k=k: e.matmul(
                        pre[0][:, t * EXPERTS:(t + 1) * EXPERTS], h_full[:, k, t * P:(t + 1) * P], router_w[:, k, :],
                        start=k == 0, stop=k == KT - 1), s_prep_pe)
            logits = pre[0][:, 0:TT * EXPERTS].rearrange("p (t x) -> p t x", x=EXPERTS)
            by_expert = lambda v: v.rearrange("p (t o) -> p t o", o=1).broadcast_to([P, TT, EXPERTS])
            dve.wait(m)
            m = dve.do(lambda e: e.tensor_reduce(neg_max[:, :], logits, AX.X, ALU.max, negate=True), s_prep_dve)
            dve.wait(m)
            m = dve.do(lambda e: e.tensor_tensor(shifted[:, :, :], logits, by_expert(neg_max[:, :]), ALU.add), s_prep_dve)
            pre_free[0] = [m]
            act.wait(m)
            m = act.do(lambda e: e.activation(exps[:, :, :], shifted[:, :, :], ACT.Exp), s_prep_act)
            dve.wait(m)
            m = dve.do(lambda e: e.tensor_reduce(exp_sum[:, :], exps[:, :, :], AX.X, ALU.add), s_prep_dve)
            dve.wait(m)
            m = dve.do(lambda e: e.reciprocal(exp_inv[:, :], exp_sum[:, :]), s_prep_dve)
            dve.wait(m)
            m = dve.do(lambda e: e.tensor_tensor(probs[:, :, 0:EXPERTS], exps[:, :, :], by_expert(exp_inv[:, :]),
                                                 ALU.mult), s_prep_dve)
            dve.wait(m, consts_in)
            for t in range(TT):
                m = dve.do(lambda e, t=t: e.max(best8[:, t, :], probs[:, t, :]), s_prep_dve)
            dve.wait(m)
            for t in range(TT):
                m = dve.do(lambda e, t=t: e.match_replace(taken[:, t, :], best8[:, t, :], probs[:, t, :], -1.0),
                           s_prep_dve)
            dve.wait(m)
            m = dve.do(lambda e: e.scalar_tensor_tensor(
                out=routing[:, :, :], in0=taken[:, :, 0:EXPERTS], scalar=0.0, in1=probs[:, :, 0:EXPERTS],
                op0=ALU.is_lt, op1=ALU.mult), s_prep_dve)
            yield
            pe.wait(m, *pre_free[1])
            for t in range(TT):
                m = pe.do(lambda e, t=t: e.transpose(pre[1][0:EXPERTS, t * P:(t + 1) * P], routing[:, t, :],
                                                     ident[:, :]), s_prep_pe)
            dve.wait(m)
            if b >= 1:
                dve.wait(routing_ready[b - 1])
            m = dve.do(lambda e: e.tensor_copy(routing_t[:, :], pre[1][0:EXPERTS, :]), s_prep_dve)
            pre_free[1] = [m]
            sp.wait(m)
            routing_ready[b] = sp.do(lambda e: e.dma_start(routing_dram[b], routing_t[:, :]), s_routing_dram, 16)

        def add_turned(rows, source, ready, s_pe, s_dve):
            pe.wait(ready)
            for half in range(2):
                pe.wait(*pre_free[half])
                for t in range(TT // 2):
                    for k in range(KT):
                        m = pe.do(lambda e, half=half, t=t, k=k: e.transpose(
                            pre[half][:, t * DIM + k * P:t * DIM + (k + 1) * P],
                            source[:, k, (half * 2 + t) * P:(half * 2 + t + 1) * P], ident[:, :]), s_pe)
                dve.wait(m)
                part = rows[:, half * 2:half * 2 + 2, :].rearrange("p t d -> p (t d)")
                m = dve.do(lambda e, half=half, part=part: e.tensor_tensor(part, part, pre[half][:, :], ALU.add), s_dve)
                pre_free[half] = [m]

        def finish(b, summed):
            for k in range(KT):
                act.wait(summed, w_out_split)
                m = act.do(lambda e, k=k: e.activation(mixed[:, k, :], sum_ps[k][:, :], ACT.Copy,
                                                       scale=mod[:, GAIN_B, k, b:b + 1]), s_fin_act)
            sums_read[b] = m
            yield
            add_turned(x_rows[b % 2], mixed, m, s_fin_pe, s_fin_dve)
            m = (s_fin_dve, counts[id(s_fin_dve)])
            sp.wait(m)
            finished[b] = sp.do(lambda e: e.dma_start(out_rows[b], x_rows[b % 2][:, :, :]), s_store[b % 2], 16)
            if b + 2 < BATCH:
                sp.wait(finished[b])
                x_loaded[b + 2] = sp.do(lambda e: e.dma_start(x_rows[b % 2][:, :, :], x_in_rows[b + 2]),
                                        s_x[b % 2], 16)

        sums_read = {}
        TOTAL = BATCH * SLOTS
        up_done, down_done, split_done, act_done, routed, silus, gated = {}, {}, {}, {}, {}, {}, {}
        row_loads = {}

        def split_slot(g):
            s = g % SLOTS
            up_raw, down_raw = w_slots[:, s, 0:UP_COLS], w_slots[:, s, UP_COLS:SLOT_COLS]
            act.wait(w_loaded[s])
            for dst_hi, dst_lo, raw, freed in (
                    (up_hi[g % 2], up_lo[g % 2], up_raw, up_done.get(g - 2)),
                    (down_hi[g % DOWN_RING], down_lo[g % DOWN_RING], down_raw, down_done.get(g - DOWN_RING))):
                if freed:
                    act.wait(freed)
                hi = act.do(lambda e, d=dst_hi, r=raw: e.copy(d[:, :], r), s_split_hi)
                pool.wait(hi)
                split_done[g] = pool.do(lambda e, d=dst_lo, h=dst_hi, r=raw: e.tensor_tensor(
                    d[:, :], r, h[:, :].bitcast(F32), ALU.subtract), s_split_lo)

        def load_rows(g):
            b, first = g // SLOTS, (g % SLOTS - SHARED_SLOTS) * P
            ring = routed_index(g) % ROUTING_RING
            sp.wait(routing_ready[b])
            before = [x for x in row_loads if row_loads[x][0] == ring]
            if before:
                sp.wait(routed[max(before)])
            at = 0
            while at < P:
                expert = (first + at) // EXPERT_HIDDEN
                to = min(P, (expert + 1) * EXPERT_HIDDEN - first)
                m = sp.do(lambda e, at=at, to=to, x=expert: e.dma_start(
                    routing_rows[ring][at:to, :], routing_dram[b, x:x + 1, :].broadcast_to([to - at, SEQ])),
                    s_rows[ring], 16)
                at = to
            row_loads[g] = (ring, m)

        def routed_index(g):
            return g // SLOTS * ROUTED_SLOTS + g % SLOTS - SHARED_SLOTS

        def is_shared(g):
            return g % SLOTS < SHARED_SLOTS

        def activate(g):
            buf, ring = hidden[g % 3], g % 2
            dve.wait(silus[g] if is_shared(g) else routed[g], up_done[g])
            m = dve.do(lambda e: e.tensor_tensor(buf[:, :], buf[:, :], up_ps[g % 2][:, :], ALU.mult), s_act)
            gated[g] = m
            act.wait(m)
            if g >= 2:
                act.wait(down_done[g - 2])
            hi = act.do(lambda e: e.copy(act_hi[ring][:, :], buf[:, :]), s_act_hi)
            dve.wait(hi)
            act_done[g] = dve.do(lambda e: e.tensor_tensor(
                act_lo[ring][:, :], buf[:, :], act_hi[ring][:, :].bitcast(F32), ALU.subtract), s_act_lo)

        def down(g):
            b, s = divmod(g, SLOTS)
            pe.wait(act_done[g], split_done[g])
            if s == 0 and b >= 1:
                pe.wait(sums_read[b - 1])
            for k in range(KT):
                hi, lo = (w[g % DOWN_RING][:, k * P:(k + 1) * P] for w in (down_hi, down_lo))
                for n, (a, v) in enumerate(((hi, act_hi), (hi, act_lo), (lo, act_hi))):
                    m = pe.do(lambda e, k=k, a=a, v=v, n=n: e.matmul(
                        sum_ps[k][:, :], a, v[g % 2][:, :], start=s == 0 and n == 0,
                        stop=s == SLOTS - 1 and n == 2), s_down_mm if (k, n) == (KT - 1, 2) else None)
            down_done[g] = m

        def up(g):
            b = g // SLOTS
            pe.wait(h_ready[b], split_done[g])
            for name, ps, part, sem_ in (("gate", gate_ps, 0, s_gate_mm), ("up", up_ps, 1, s_up_mm)):
                if g >= 2:
                    pe.wait(gated[g - 2] if name == "up" else silus[g - 2])
                pairs = []
                for k in range(KT):
                    cols = slice((2 * k + part) * P, (2 * k + part + 1) * P)
                    pairs.append(((up_hi[g % 2][:, cols], up_lo[g % 2][:, cols]),
                                  (h_hi[b % 2][:, k, :], h_lo[b % 2][:, k, :])))
                m = split_products(ps[g % 2][:, :], pairs, sem_)
                if name == "gate":
                    gate_done = m
            up_done[g] = m
            if g % SLOTS == SLOTS - 1:
                block_up_done[b] = m
            return gate_done

        for _ in prepare(0):
            pass
        split_slot(0)
        preparing, finishing = iter(()), iter(())
        for g in range(TOTAL + DOWN_LAG):
            b, s = divmod(g, SLOTS)
            if g + 1 < TOTAL:
                split_slot(g + 1)
            if g - 1 >= 0 and g - 1 < TOTAL:
                activate(g - 1)
            if g < TOTAL:
                if s == PREPARE_FROM_SLOT and b + 1 < BATCH:
                    preparing = prepare(b + 1)
                gate_done = up(g)
                if not is_shared(g):
                    load_rows(g)
                buf = hidden[g % 3]
                act.wait(gate_done)
                m = act.do(lambda e, g=g, buf=buf: e.activation(buf[:, :], gate_ps[g % 2][:, :], ACT.Tanh,
                                                                scale=0.5), s_tanh)
                dve.wait(m)
                silus[g] = dve.do(lambda e, g=g, buf=buf: e.scalar_tensor_tensor(
                    out=buf[:, :], in0=buf[:, :], scalar=1.0, in1=gate_ps[g % 2][:, :],
                    op0=ALU.add, op1=ALU.mult), s_silu)
                if not is_shared(g):
                    ring, rows_in = row_loads[g]
                    pool.wait(silus[g], rows_in)
                    routed[g] = pool.do(lambda e, buf=buf, ring=ring: e.tensor_tensor(
                        buf[:, :], buf[:, :], routing_rows[ring][:, :], ALU.mult), s_routed)
            if g >= DOWN_LAG:
                down(g - DOWN_LAG)
                if (g - DOWN_LAG) % SLOTS == SLOTS - 1:
                    finishing = finish((g - DOWN_LAG) // SLOTS, down_done[g - DOWN_LAG])
            next(finishing, None)
            next(preparing, None)
        for _ in finishing:
            pass
        for b in range(BATCH):
            sp.wait(finished[b])

        block = ctx.enter_context(nc.Block())
        block.sync(sp.play)
        block.tensor(pe.play)
        block.scalar(act.play)
        block.vector(dve.play)
        block.gpsimd(pool.play)


def slot_weights(gate, up, down):
    rows = gate.shape[0]
    slots = -(-rows // P)
    laid = np.zeros((P, slots, SLOT_COLS), gate.dtype)
    for s in range(slots):
        n = min(P, rows - s * P)
        part = slice(s * P, s * P + n)
        for k in range(KT):
            for j, w in enumerate((gate, up)):
                at = (2 * k + j) * P
                laid[:, s, at:at + n] = w[part, k * P:(k + 1) * P].T
        laid[:n, s, UP_COLS:] = down[:, part].T
    return laid


def kernel(**inputs):
    import concourse.bacc as _bacc
    from concourse.bass_utils import run_bass_kernel_spmd as _run

    a = {n.removeprefix("L0_"): np.asarray(v) for n, v in inputs.items()}
    w1, w2 = a["ffn_w1"], a["ffn_w2"]
    shared1, shared2 = a["ffn_shared_w1"], a["ffn_shared_w2"]
    gates = a["attn_W_gate"].reshape(HEADS, 4, HEAD_DIM, DIM)
    arrays = {
        "x": a["attn_x"],
        "w_in": a["attn_W_in"],
        "w_gate_t": gates.transpose(3, 1, 0, 2).reshape(DIM, 4 * DIM),
        "b_gate": a["attn_b_gate"].reshape(HEADS, 4, HEAD_DIM).transpose(1, 0, 2).reshape(4 * KT, P).T,
        "rms_w": a["attn_rms_w"].reshape(HEAD_DIM, 1),
        "w_out_t": a["attn_W_out"].T,
        "router_t": a["ffn_gate_w"].T,
        "shared_w": slot_weights(shared1[:SHARED_HIDDEN], shared1[SHARED_HIDDEN:], shared2),
        "routed_w": slot_weights(w1[:, :EXPERT_HIDDEN].reshape(-1, DIM), w1[:, EXPERT_HIDDEN:].reshape(-1, DIM),
                                 w2.transpose(1, 0, 2).reshape(DIM, -1)),
        "cond_t": a["c"].T,
        "w_mod": a["wmod"],
    }
    arrays = {n: np.ascontiguousarray(v) for n, v in arrays.items()}
    nc = _bacc.Bacc("TRN2", target_bir_lowering=False, num_devices=1)
    args = [nc.dram_tensor(n, v.shape, mybir.dt.from_np(v.dtype), kind="ExternalInput").ap()
            for n, v in arrays.items()]
    args.append(nc.dram_tensor("out", (BATCH, SEQ, DIM), F32, kind="ExternalOutput").ap())
    adaln_program(nc, *args)
    return _run(nc, [arrays], core_ids=[0]).results[0]["out"]
```

```python
from contextlib import ExitStack
from itertools import chain

import numpy as np

import concourse.bass as bass
from concourse import mybir

F32 = mybir.dt.float32
F32R = mybir.dt.float32r
I32 = mybir.dt.int32
ALU = mybir.AluOpType
ACT = mybir.ActivationFunctionType
AX = mybir.AxisListType

P = 128
BATCH, SEQ, DIM = 4, 512, 256
HEADS, HEAD_DIM = 4, 64
EXPERTS, EXPERT_HIDDEN, TOP_K = 16, 176, 6
SHARED_HIDDEN = 352
LN_EPS, RMS_EPS, GATE_FLOOR = 1e-5, 1e-6, 0.25

KT = DIM // P
TT = SEQ // P
GATE_C, GATE_I, GATE_F, GATE_O = range(4)
REFERENCE_GATES = (3, 0, 1, 2)
HEADS_PER_TILE = P // HEAD_DIM
SHARED_SLOTS = -(-SHARED_HIDDEN // P)
ROUTED_SLOTS = EXPERTS * EXPERT_HIDDEN // P
SLOTS = SHARED_SLOTS + ROUTED_SLOTS
UP_COLS = KT * 2 * P
SLOT_COLS = UP_COLS + DIM
SHIFT_A, SCALE_A, GAIN_A, SHIFT_B, SCALE_B, GAIN_B = range(6)
MODS = 6
MAX8 = 8
BIG_PROB = 2.0
RSQRT_SEED = float(0x5F3759DF)
DOWN_LAG = 2
ROUTING_RING = 4
DOWN_RING = 4
X_RING = 3
PREPARE_AHEAD = 3
STAGING_SLOT = SLOTS - KT * (MODS + 4) * DIM // SLOT_COLS - 1


class Engine:

    def __init__(self, counts):
        self.steps, self.counts, self.waited, self.between = [], counts, {}, []

    def wait(self, *marks):
        for sem, value in marks:
            if self.waited.get(id(sem), 0) < value:
                self.waited[id(sem)] = value
                self.steps.append(lambda e, s=sem, v=value: e.wait_ge(s, v))

    def do(self, step, sem=None, by=1):
        if sem is None:
            self.steps.append(step)
            mark = None
        else:
            self.counts[id(sem)] = self.counts.get(id(sem), 0) + by
            self.steps.append(lambda e: step(e).then_inc(sem, by))
            mark = (sem, self.counts[id(sem)])
        if self.between:
            self.place_one()
        return mark

    def chain(self, first, steps, sem):
        self.place_all()
        for step in steps:
            self.counts[id(sem)] = self.counts.get(id(sem), 0) + 1
            self.between.append((first, step, sem))
            first = (sem, self.counts[id(sem)])
        return first

    def place_one(self):
        before, step, sem = self.between.pop(0)
        self.wait(before)
        self.steps.append(lambda e: step(e).then_inc(sem, 1))

    def place_all(self):
        while self.between:
            self.place_one()

    def play(self, e):
        for step in self.steps:
            step(e)


def adaln_program(nc, x_in, w_in, w_gate_t, b_gate, rms_w, w_out_t, router_t, shared_w, routed_w,
                  cond_t, w_mod, out):
    ctx = ExitStack()
    with ctx:
        def sb(name, shape, dt=F32):
            return ctx.enter_context(nc.sbuf_tensor(name, shape, dt))

        def sem(name):
            return ctx.enter_context(nc.semaphore(name))

        routing_dram = nc.dram_tensor("routing_dram", [BATCH, EXPERTS, SEQ], F32, kind="Internal").ap()

        ident = sb("ident", [P, P])
        head_mean = sb("head_mean", [P, HEADS_PER_TILE])
        w_slots = sb("w_slots", [P, SLOTS, SLOT_COLS])
        w_gates_hi = sb("w_gates_hi", [P, KT, 4 * DIM], F32R)
        w_gates_lo = sb("w_gates_lo", [P, KT, 4 * DIM], F32R)
        w_out_hi = sb("w_out_hi", [P, KT, DIM], F32R)
        w_out_lo = sb("w_out_lo", [P, KT, DIM], F32R)
        router_w = sb("router_w", [P, KT, EXPERTS])
        gate_bias = sb("gate_bias", [P, 4 * KT])
        half_bias = sb("half_bias", [P, 4 * KT])
        rms_scale = sb("rms_scale", [P, 1])
        cond = sb("cond", [P, KT, BATCH])
        cond_tanh = sb("cond_tanh", [P, KT, BATCH])
        cond_silu = sb("cond_silu", [P, KT, BATCH])
        mod = sb("mod", [P, MODS, KT, BATCH])
        gain_sign = sb("gain_sign", [P, KT, BATCH])
        gain_abs = sb("gain_abs", [P, KT, BATCH])

        x_rows = [sb(f"x_rows{i}", [P, TT, DIM]) for i in range(X_RING)]
        h_hi = [sb(f"h_hi{i}", [P, KT, SEQ], F32R) for i in range(2)]
        h_lo = [sb(f"h_lo{i}", [P, KT, SEQ], F32R) for i in range(2)]
        work = sb("work", [P, 5, KT, SEQ])
        gate_i, gate_c, gate_f, gate_o, cell = (work[:, n] for n in range(5))
        mixed = sb("mixed", [P, KT, SEQ])
        cell_out_hi = sb("cell_out_hi", [P, KT, SEQ], F32R)
        cell_out_lo = sb("cell_out_lo", [P, KT, SEQ], F32R)
        h_full = gate_i
        normed = work[:, 1].rearrange("p k t -> p (k t)").rearrange("p (t d) -> p t d", d=DIM)
        square, cell_tanh = gate_c, gate_c
        inv_rms_wide = work[:, 2].rearrange("p k t -> p (k t)").rearrange("p (k t c) -> p k t c", k=KT, c=P)
        cell_out = gate_i
        projected = cell
        tail = w_slots[:, STAGING_SLOT:SLOTS, :].rearrange("p s c -> p (s c)")
        w_mod_raw = tail[:, 0:KT * MODS * DIM].rearrange("p (k m) -> p k m", k=KT)
        w_gate_raw = tail[:, KT * MODS * DIM:KT * (MODS + 4) * DIM].rearrange("p (k m) -> p k m", k=KT)
        mixed_flat = mixed[:, :, :].rearrange("p k t -> p (k t)")
        w_in_raw = mixed_flat[:, 0:KT * DIM].rearrange("p (k m) -> p k m", k=KT)
        w_out_raw = mixed_flat[:, KT * DIM:2 * KT * DIM].rearrange("p (k m) -> p k m", k=KT)

        stats = sb("stats", [P, TT, 6])
        mean_var = sb("mean_var", [P, TT, 2])
        ln_in = sb("ln_in", [P, TT])
        ln_seed = sb("ln_seed", [P, TT], I32)
        ln_y = sb("ln_y", [P, TT], I32)
        ln_t = sb("ln_t", [P, TT])
        NORMS = KT * TT * HEADS_PER_TILE
        rms_in = sb("rms_in", [P, NORMS])
        rms_seed = sb("rms_seed", [P, NORMS], I32)
        rms_y = sb("rms_y", [P, NORMS], I32)
        rms_t = sb("rms_t", [P, NORMS])
        neg_max = sb("neg_max", [P, TT])
        shifted = sb("shifted", [P, TT, EXPERTS])
        exps = sb("exps", [P, TT, EXPERTS])
        exp_sum = sb("exp_sum", [P, TT])
        exp_inv = sb("exp_inv", [P, TT])
        PADDED = EXPERTS + MAX8 - TOP_K
        probs = sb("probs", [P, TT, PADDED])
        best8 = sb("best8", [P, TT, MAX8])
        taken = sb("taken", [P, TT, PADDED])
        routing = sb("routing", [P, TT, EXPERTS])
        routing_t = sb("routing_t", [EXPERTS, SEQ])

        up_hi = [sb(f"up_hi{i}", [P, UP_COLS], F32R) for i in range(2)]
        up_lo = [sb(f"up_lo{i}", [P, UP_COLS], F32R) for i in range(2)]
        down_hi = [sb(f"down_hi{i}", [P, DIM], F32R) for i in range(DOWN_RING)]
        down_lo = [sb(f"down_lo{i}", [P, DIM], F32R) for i in range(DOWN_RING)]
        hidden = [sb(f"hidden{i}", [P, SEQ]) for i in range(3)]
        act_hi = [sb(f"act_hi{i}", [P, SEQ], F32R) for i in range(2)]
        act_lo = [sb(f"act_lo{i}", [P, SEQ], F32R) for i in range(2)]
        routing_rows = [sb(f"routing_rows{i}", [P, SEQ]) for i in range(ROUTING_RING)]

        def bank(name):
            return ctx.enter_context(nc.psum_tensor(name, [P, SEQ], F32))

        pre = [bank(f"pre{i}") for i in range(2)]
        gate_ps = [bank(f"gate_ps{i}") for i in range(2)]
        up_ps = [bank(f"up_ps{i}") for i in range(2)]
        sum_ps = [bank(f"sum_ps{i}") for i in range(KT)]

        counts = {}
        sp, pe, act, dve, pool = (Engine(counts) for _ in range(5))

        s_load = {n: sem(f"s_load_{n}") for n in
                  ("first_mods", "other_mods", "cond", "w_gate", "w_in", "w_out", "small", "router")}
        s_x = [sem(f"s_x{i}") for i in range(X_RING)]
        W_PARTS = [(0, 1), (1, 3), (3, 7), (7, 12), (12, STAGING_SLOT), (STAGING_SLOT, SLOTS)]
        s_w = [sem(f"s_w{i}") for i in range(len(W_PARTS))]
        s_store = [sem(f"s_store{i}") for i in range(X_RING)]
        s_routing_dram = sem("s_routing_dram")
        s_rows = [sem(f"s_rows{i}") for i in range(ROUTING_RING)]
        s_rsqrt = sem("s_rsqrt")
        s_const, s_setup_act, s_setup_dve, s_setup_pe = (sem(n) for n in (
            "s_const", "s_setup_act", "s_setup_dve", "s_setup_pe"))
        s_prep_pe, s_prep_act, s_prep_dve, s_prep_pool = (sem(n) for n in (
            "s_prep_pe", "s_prep_act", "s_prep_dve", "s_prep_pool"))
        s_fin_pe, s_fin_act, s_fin_dve = (sem(n) for n in ("s_fin_pe", "s_fin_act", "s_fin_dve"))
        s_gate_mm, s_up_mm, s_down_mm = (sem(n) for n in ("s_gate_mm", "s_up_mm", "s_down_mm"))
        s_split_hi, s_up_lo, s_down_lo = sem("s_split_hi"), sem("s_up_lo"), sem("s_down_lo")
        s_tanh, s_silu, s_routed, s_act, s_act_hi, s_act_lo = (sem(n) for n in (
            "s_tanh", "s_silu", "s_routed", "s_act", "s_act_hi", "s_act_lo"))

        def split_products(dst, pairs, sem_=None):
            last, n = None, 0
            for (a_hi, a_lo), (b_hi, b_lo) in pairs:
                for a, b in ((a_hi, b_hi), (a_hi, b_lo), (a_lo, b_hi)):
                    n += 1
                    first, end = n == 1, n == 3 * len(pairs)
                    last = pe.do(lambda e, a=a, b=b, f=first, l=end: e.matmul(dst, a, b, start=f, stop=l),
                                 sem_ if end else None)
            return last

        def load(queue, dst, src, sem_):
            return queue.do(lambda e: e.dma_start(dst, src), sem_, 16)

        x_in_rows = x_in.rearrange("b (t p) d -> b p t d", p=P)
        out_rows = out.rearrange("b (t p) d -> b p t d", p=P)
        x_loaded = {0: load(sp, x_rows[0][:, :, :], x_in_rows[0], s_x[0])}
        w_mod_rows = w_mod.rearrange("(k p) m -> p k m", p=P)
        FIRST_MODS = (SCALE_A + 1) * DIM
        cond_in = load(act, cond[:, :, :], cond_t.rearrange("(k p) b -> p k b", p=P), s_load["cond"])
        first_mods_in = load(act, w_mod_raw[:, :, 0:FIRST_MODS], w_mod_rows[:, :, 0:FIRST_MODS], s_load["first_mods"])
        w_in_in = load(sp, w_in_raw, w_in.rearrange("(k p) m -> p k m", p=P), s_load["w_in"])
        w_gate_in = load(sp, w_gate_raw, w_gate_t.rearrange("(k p) m -> p k m", p=P), s_load["w_gate"])
        load(sp, gate_bias[:, :], b_gate, s_load["small"])
        for h in range(HEADS_PER_TILE):
            small_in = load(sp, rms_scale[h * HEAD_DIM:(h + 1) * HEAD_DIM, :], rms_w, s_load["small"])
        other_mods_in = load(sp, w_mod_raw[:, :, FIRST_MODS:], w_mod_rows[:, :, FIRST_MODS:], s_load["other_mods"])
        w_out_in = load(sp, w_out_raw, w_out_t.rearrange("(k p) m -> p k m", p=P), s_load["w_out"])
        router_in = load(sp, router_w[:, :, :], router_t.rearrange("(k p) m -> p k m", p=P), s_load["router"])
        w_loaded = {}

        def load_slots(i):
            a, b = W_PARTS[i]
            src = shared_w[:, a:b, :] if b <= SHARED_SLOTS else routed_w[:, a - SHARED_SLOTS:b - SHARED_SLOTS, :]
            mark = load(sp, w_slots[:, a:b, :], src, s_w[i])
            for s in range(a, b):
                w_loaded[s] = mark

        for i in range(2):
            load_slots(i)
        x_loaded[1] = load(sp, x_rows[1][:, :, :], x_in_rows[1], s_x[1])
        for i in range(2, len(W_PARTS) - 1):
            load_slots(i)
        x_loaded[2] = load(sp, x_rows[2][:, :, :], x_in_rows[2], s_x[2])

        pool.do(lambda e: e.memset(ident[:, :], 0.0), s_const)
        pool.do(lambda e: e.memset(head_mean[:, :], 0.0), s_const)
        zeroed = pool.do(lambda e: e.memset(probs[:, :, EXPERTS:PADDED], BIG_PROB), s_const)
        pool.wait(zeroed)
        consts_in = pool.do(lambda e: e.affine_select(out=ident[:, :], in_=ident[:, :], compare_op=ALU.not_equal, fill=1.0,
                                          base=0, pattern=[[-1, P]], channel_multiplier=1), s_const)
        for h in range(HEADS_PER_TILE):
            pool.wait(consts_in)
            consts_in = pool.do(lambda e, h=h: e.memset(
                head_mean[h * HEAD_DIM:(h + 1) * HEAD_DIM, h:h + 1], 1.0 / HEAD_DIM), s_const)

        pool.wait(consts_in)
        act.wait(cond_in)
        m = act.do(lambda e: e.activation(cond_tanh[:, :, :], cond[:, :, :], ACT.Tanh, scale=0.5), s_setup_act)
        dve.wait(m)
        silu2 = dve.do(lambda e: e.scalar_tensor_tensor(
            out=cond_silu[:, :, :], in0=cond_tanh[:, :, :], scalar=1.0, in1=cond[:, :, :],
            op0=ALU.add, op1=ALU.mult), s_setup_dve)
        pe.wait(silu2, consts_in)
        mod_ps = sum_ps[0][:, 0:MODS * KT * BATCH]

        mod_read = []

        def modulation(first, last):
            pe.wait(*mod_read)
            for n in range(first * KT, last * KT):
                for k in range(KT):
                    m = pe.do(lambda e, n=n, k=k: e.matmul(
                        mod_ps[:, n * BATCH:(n + 1) * BATCH], w_mod_raw[:, k, n * P:(n + 1) * P],
                        cond_silu[:, k, :], start=k == 0, stop=k == KT - 1), s_setup_pe)
            dve.wait(m)
            m = dve.do(lambda e: e.tensor_scalar(
                mod[:, first:last], mod_ps[:, first * KT * BATCH:last * KT * BATCH].rearrange(
                    "p (m k b) -> p m k b", m=last - first, k=KT), 0.5, None, ALU.mult), s_setup_dve)
            mod_read[:] = [m]
            dve.wait(m)
            return m

        def one_plus(i):
            m = dve.do(lambda e: e.tensor_scalar(mod[:, i], mod[:, i], 1.0, None, ALU.add), s_setup_dve)
            dve.wait(m)
            return m

        def floored_gain(i):
            m = dve.do(lambda e: e.tensor_scalar(gain_sign[:, :, :], mod[:, i], 0.0, 2.0, ALU.is_ge, ALU.mult),
                       s_setup_dve)
            dve.wait(m)
            m = dve.do(lambda e: e.tensor_scalar(gain_sign[:, :, :], gain_sign[:, :, :], -1.0, None, ALU.add),
                       s_setup_dve)
            dve.wait(m)
            m = dve.do(lambda e: e.tensor_tensor(gain_abs[:, :, :], mod[:, i], gain_sign[:, :, :], ALU.mult),
                       s_setup_dve)
            dve.wait(m)
            m = dve.do(lambda e: e.tensor_scalar(gain_abs[:, :, :], gain_abs[:, :, :], GATE_FLOOR, 0.5,
                                                 ALU.max, ALU.mult), s_setup_dve)
            dve.wait(m)
            m = dve.do(lambda e: e.tensor_tensor(mod[:, i], gain_abs[:, :, :], gain_sign[:, :, :], ALU.mult),
                       s_setup_dve)
            dve.wait(m)
            return m

        pe.wait(first_mods_in)
        modulation(SHIFT_A, SCALE_A + 1)
        first_mods_ready = one_plus(SCALE_A)
        dve.wait(small_in)
        bias_ready = dve.do(lambda e: e.tensor_scalar(half_bias[:, :], gate_bias[:, :], 0.5, None, ALU.mult),
                            s_setup_dve)

        w_gates_ready = {}
        combined_ps = [gate_ps[0], gate_ps[1], up_ps[0], up_ps[1]]

        def combine_weights():
            pe.wait(w_in_in, w_gate_in)
            for n, (half, k) in enumerate((half, k) for half in range(2) for k in range(KT)):
                cols = slice(half * SEQ, (half + 1) * SEQ)
                for kk in range(KT):
                    m = pe.do(lambda e, n=n, k=k, kk=kk, cols=cols: e.matmul(
                        combined_ps[n][:, :], w_in_raw[:, kk, k * P:(k + 1) * P], w_gate_raw[:, kk, cols],
                        start=kk == 0, stop=kk == KT - 1), s_setup_pe)
                act.wait(m)
                hi = act.do(lambda e, n=n, k=k, cols=cols: e.copy(w_gates_hi[:, k, cols], combined_ps[n][:, :]),
                            s_setup_act)
                dve.wait(hi)
                w_gates_ready[half] = dve.do(lambda e, n=n, k=k, cols=cols: e.tensor_tensor(
                    w_gates_lo[:, k, cols], combined_ps[n][:, :], w_gates_hi[:, k, cols].bitcast(F32),
                    ALU.subtract), s_setup_dve)

        def other_setup():
            pe.wait(other_mods_in)
            modulation(GAIN_A, GAIN_A + 1)
            prepared[GAIN_A] = floored_gain(GAIN_A)
            yield
            modulation(SHIFT_B, SCALE_B + 1)
            prepared[SCALE_B] = one_plus(SCALE_B)
            yield
            modulation(GAIN_B, MODS)
            prepared[GAIN_B] = floored_gain(GAIN_B)
            sp.wait(prepared[GAIN_B])
            load_slots(len(W_PARTS) - 1)

        prepared = {}
        act.wait(w_out_in)
        hi = act.do(lambda e: e.copy(w_out_hi[:, :, :], w_out_raw), s_setup_act)
        pool.wait(hi)
        w_out_ready = pool.do(lambda e: e.tensor_tensor(
            w_out_lo[:, :, :], w_out_raw, w_out_hi[:, :, :].bitcast(F32), ALU.subtract), s_const)
        pre_free = [[], []]

        def rsqrt(value, ready, seed, y, tmp):
            yf = y.bitcast(F32)
            newton = [
                lambda e: e.tensor_tensor(tmp, value, yf, ALU.mult),
                lambda e: e.scalar_tensor_tensor(out=tmp, in0=tmp, scalar=-0.5, in1=yf, op0=ALU.mult, op1=ALU.mult),
                lambda e: e.scalar_tensor_tensor(out=yf, in0=tmp, scalar=1.5, in1=yf, op0=ALU.add, op1=ALU.mult)]
            return dve.chain(ready, [
                lambda e: e.tensor_scalar(seed, value.bitcast(I32), 1, None, ALU.logical_shift_right),
                lambda e: e.tensor_scalar(y, seed, -1.0, RSQRT_SEED, ALU.mult, ALU.add)] + 3 * newton, s_rsqrt)

        def norm_rows(rows, ready):
            dve.wait(*ready)
            for t in range(TT):
                m = dve.do(lambda e, t=t: e.bn_stats(stats[:, t, :], rows[:, t, :]), s_prep_dve)
            dve.wait(m)
            dve.wait(m)
            for t in range(TT):
                m = dve.do(lambda e, t=t: e.bn_aggr(mean_var[:, t, :], stats[:, t, :]), s_prep_dve)
            dve.wait(m)
            m = dve.do(lambda e: e.tensor_scalar(ln_in[:, :], mean_var[:, :, 1], LN_EPS, None, ALU.add), s_prep_dve)
            m = rsqrt(ln_in[:, :], m, ln_seed[:, :], ln_y[:, :], ln_t[:, :])
            yield
            yield
            dve.place_all()
            dve.wait(m)
            inv = ln_y[:, :].bitcast(F32)
            for t in range(TT):
                m = dve.do(lambda e, t=t: e.tensor_scalar(
                    normed[:, t, :], rows[:, t, :], mean_var[:, t, 0:1], inv[:, t:t + 1],
                    ALU.subtract, ALU.mult), s_prep_dve)
            yield
            return m

        def split_rows(hi, lo, full, ready, hi_free):
            dve.wait(ready, *hi_free)
            his = [dve.do(lambda e, k=k: e.tensor_copy(hi[:, k, :], full[:, k, :]), s_prep_dve) for k in range(KT)]
            los = []
            for k, (queue, sem_) in enumerate(((dve, s_prep_dve), (pool, s_prep_pool))):
                queue.wait(his[k])
                los.append(queue.do(lambda e, k=k: e.tensor_tensor(
                    lo[:, k, :], full[:, k, :], hi[:, k, :].bitcast(F32), ALU.subtract), sem_))
            return los

        def turn_and_modulate(b, normed_ready, mods_ready, scale, shift, h, h_users):
            pe.wait(normed_ready, consts_in)
            for k in range(KT):
                pe.wait(*pre_free[k])
                for t in range(TT):
                    m = pe.do(lambda e, k=k, t=t: e.transpose(
                        pre[k][:, t * P:(t + 1) * P], normed[:, t, k * P:(k + 1) * P], ident[:, :]),
                        s_prep_pe if t == TT - 1 else None)
                act.wait(m, mods_ready)
                full = act.do(lambda e, k=k: e.activation(
                    h_full[:, k, :], pre[k][:, :], ACT.Identity, bias=mod[:, shift, k, b:b + 1],
                    scale=mod[:, scale, k, b:b + 1]), s_prep_act)
                pre_free[k] = [full]
            yield
            los = split_rows(h_hi[h], h_lo[h], h_full, full, h_users())
            return full, los

        block_up_done = {}
        finished = {}
        h_ready = {}
        routing_ready = {}

        def prepare(b):
            rows, h = x_rows[b % X_RING], b % 2
            h_users = lambda: [block_up_done[b - 2]] if b >= 2 else []
            m = yield from norm_rows(rows, [x_loaded[b]])
            if b == 0:
                combine_weights()
            full, los = yield from turn_and_modulate(b, m, first_mods_ready, SCALE_A, SHIFT_A, h, h_users)

            def gate(p, which, k, dst, func, scale, bias):
                n = which * KT + k
                cols = slice(n * P, (n + 1) * P)
                pe.wait(w_gates_ready[which // 2], *pre_free[p])
                mm = split_products(pre[p][:, :], [
                    ((w_gates_hi[:, kk, cols], w_gates_lo[:, kk, cols]),
                     (h_hi[h][:, kk, :], h_lo[h][:, kk, :])) for kk in range(KT)], s_prep_pe)
                act.wait(mm, bias_ready)
                done = act.do(lambda e: e.activation(dst[:, k, :], pre[p][:, :], func, bias=bias[:, n:n + 1],
                                                     scale=scale), s_prep_act)
                pre_free[p] = [done]
                return mm, done

            def input_gates(k):
                _, c = gate(0, GATE_C, k, gate_c, ACT.Tanh, 1.0, gate_bias)
                _, i = gate(1, GATE_I, k, gate_i, ACT.Exp, 1.0, gate_bias)
                return c, i

            def other_gates(k):
                _, f = gate(0, GATE_F, k, gate_f, ACT.Tanh, 0.5, half_bias)
                mm, o = gate(1, GATE_O, k, gate_o, ACT.Tanh, 0.5, half_bias)
                return mm, f, o

            def gated_input(k, c, i):
                pool.wait(c, i)
                return pool.do(lambda e: e.tensor_tensor(gate_i[:, k, :], gate_i[:, k, :], gate_c[:, k, :],
                                                         ALU.mult), s_prep_pool)

            def recurrence(k, f, gated_in):
                dve.wait(f)
                m = dve.do(lambda e: e.tensor_scalar(gate_f[:, k, :], gate_f[:, k, :], 0.5, 0.5,
                                                     ALU.mult, ALU.add), s_prep_dve)
                dve.wait(m, gated_in)
                m = dve.do(lambda e: e.tensor_tensor_scan(
                    cell[:, k, :], gate_f[:, k, :], gate_i[:, k, :], 0.0, ALU.mult, ALU.add), s_prep_dve)
                act.wait(m)
                return act.do(lambda e: e.activation(square[:, k, :], cell[:, k, :], ACT.Square), s_prep_act)

            def mean_squares(k, squared):
                pe.wait(squared)
                if k == 0:
                    pe.wait(*pre_free[0])
                for t in range(TT):
                    at = (k * TT + t) * HEADS_PER_TILE
                    m = pe.do(lambda e, t=t, at=at: e.matmul(
                        pre[0][:, at:at + HEADS_PER_TILE], square[:, k, t * P:(t + 1) * P], head_mean[:, :],
                        start=True, stop=True), s_prep_pe)
                return m

            yield
            pe.wait(*los)
            c0, i0 = input_gates(0)
            yield
            gated0 = gated_input(0, c0, i0)
            _, f0, o0 = other_gates(0)
            yield
            squared0 = recurrence(0, f0, gated0)
            c1, i1 = input_gates(1)
            yield
            gated1 = gated_input(1, c1, i1)
            gates_done, f1, o1 = other_gates(1)
            yield
            mean_squares(0, squared0)
            squared1 = recurrence(1, f1, gated1)
            if b == 0:
                other = other_setup()
                next(other)
            yield
            m = mean_squares(1, squared1)
            dve.wait(m)
            m = dve.do(lambda e: e.tensor_scalar(rms_in[:, :], pre[0][:, 0:NORMS], RMS_EPS, None, ALU.add), s_prep_dve)
            pre_free[0] = [m]
            if b == 0:
                next(other)
            m = rsqrt(rms_in[:, :], m, rms_seed[:, :], rms_y[:, :], rms_t[:, :])
            yield
            yield
            dve.place_all()
            dve.wait(m)
            inv = rms_y[:, :].bitcast(F32).rearrange("p (n o) -> p n o", o=1)
            wide = inv_rms_wide.rearrange("p k t c -> p (k t c)").rearrange("p (n d) -> p n d", d=HEAD_DIM)
            spread = dve.do(lambda e: e.tensor_copy(wide, inv.broadcast_to([P, NORMS, HEAD_DIM])), s_prep_dve)
            yield
            pe.wait(spread)
            scaled = []
            for k in range(KT):
                pe.wait(*pre_free[k])
                for t in range(TT):
                    m = pe.do(lambda e, k=k, t=t: e.transpose(pre[k][:, t * P:(t + 1) * P],
                                                              inv_rms_wide[:, k, t, :], ident[:, :]), s_prep_pe)
                dve.wait(m)
                m = dve.do(lambda e, k=k: e.tensor_tensor(cell[:, k, :], cell[:, k, :], pre[k][:, :], ALU.mult),
                           s_prep_dve)
                pre_free[k] = [m]
                scaled.append(m)
            if b == 0:
                next(other, None)
            yield
            for k, o in enumerate((o0, o1)):
                act.wait(scaled[k])
                m = act.do(lambda e, k=k: e.activation(cell_tanh[:, k, :], cell[:, k, :], ACT.Tanh,
                                                       scale=rms_scale[:, 0:1]), s_prep_act)
                dve.wait(m, o)
                m = dve.do(lambda e, k=k: e.scalar_tensor_tensor(
                    out=cell_out[:, k, :], in0=gate_o[:, k, :], scalar=1.0, in1=cell_tanh[:, k, :],
                    op0=ALU.add, op1=ALU.mult), s_prep_dve)
            yield
            los = split_rows(cell_out_hi, cell_out_lo, cell_out, m, [])
            yield
            pe.wait(w_out_ready, *los)
            for k in range(KT):
                pe.wait(*pre_free[k])
                m = split_products(pre[k][:, :], [
                    ((w_out_hi[:, kk, k * P:(k + 1) * P], w_out_lo[:, kk, k * P:(k + 1) * P]),
                     (cell_out_hi[:, kk, :], cell_out_lo[:, kk, :])) for kk in range(KT)], s_prep_pe)
                act.wait(m, prepared[GAIN_A])
                m = act.do(lambda e, k=k: e.activation(projected[:, k, :], pre[k][:, :], ACT.Copy,
                                                       scale=mod[:, GAIN_A, k, b:b + 1]), s_prep_act)
                pre_free[k] = [m]
            yield
            m = add_turned(rows, projected, m, s_prep_pe, s_prep_dve)
            m = yield from norm_rows(rows, [m])
            full, los = yield from turn_and_modulate(b, m, prepared[SCALE_B], SCALE_B, SHIFT_B, h, lambda: [gates_done])
            h_ready[b] = los
            yield
            pe.wait(full, router_in, *pre_free[0])
            for t in range(TT):
                for k in range(KT):
                    m = pe.do(lambda e, t=t, k=k: e.matmul(
                        pre[0][:, t * EXPERTS:(t + 1) * EXPERTS], h_full[:, k, t * P:(t + 1) * P], router_w[:, k, :],
                        start=k == 0, stop=k == KT - 1), s_prep_pe)
            logits = pre[0][:, 0:TT * EXPERTS].rearrange("p (t x) -> p t x", x=EXPERTS)
            by_expert = lambda v: v.rearrange("p (t o) -> p t o", o=1).broadcast_to([P, TT, EXPERTS])
            dve.wait(m)
            m = dve.do(lambda e: e.tensor_reduce(neg_max[:, :], logits, AX.X, ALU.max, negate=True), s_prep_dve)
            dve.wait(m)
            m = dve.do(lambda e: e.tensor_tensor(shifted[:, :, :], logits, by_expert(neg_max[:, :]), ALU.add), s_prep_dve)
            pre_free[0] = [m]
            act.wait(m)
            m = act.do(lambda e: e.activation(exps[:, :, :], shifted[:, :, :], ACT.Exp), s_prep_act)
            yield
            dve.wait(m)
            m = dve.do(lambda e: e.tensor_reduce(exp_sum[:, :], exps[:, :, :], AX.X, ALU.add), s_prep_dve)
            dve.wait(m)
            m = dve.do(lambda e: e.reciprocal(exp_inv[:, :], exp_sum[:, :]), s_prep_dve)
            dve.wait(m)
            m = dve.do(lambda e: e.tensor_tensor(probs[:, :, 0:EXPERTS], exps[:, :, :], by_expert(exp_inv[:, :]),
                                                 ALU.mult), s_prep_dve)
            dve.wait(m, consts_in)
            for t in range(TT):
                m = dve.do(lambda e, t=t: e.max(best8[:, t, :], probs[:, t, :]), s_prep_dve)
            dve.wait(m)
            yield
            for t in range(TT):
                m = dve.do(lambda e, t=t: e.match_replace(taken[:, t, :], best8[:, t, :], probs[:, t, :], -1.0),
                           s_prep_dve)
            dve.wait(m)
            m = dve.do(lambda e: e.scalar_tensor_tensor(
                out=routing[:, :, :], in0=taken[:, :, 0:EXPERTS], scalar=0.0, in1=probs[:, :, 0:EXPERTS],
                op0=ALU.is_lt, op1=ALU.mult), s_prep_dve)
            yield
            pe.wait(m, *pre_free[1])
            for t in range(TT):
                m = pe.do(lambda e, t=t: e.transpose(pre[1][0:EXPERTS, t * P:(t + 1) * P], routing[:, t, :],
                                                     ident[:, :]), s_prep_pe)
            dve.wait(m)
            if b >= 1:
                dve.wait(routing_ready[b - 1])
            m = dve.do(lambda e: e.tensor_copy(routing_t[:, :], pre[1][0:EXPERTS, :]), s_prep_dve)
            pre_free[1] = [m]
            sp.wait(m)
            routing_ready[b] = sp.do(lambda e: e.dma_start(routing_dram[b], routing_t[:, :]), s_routing_dram, 16)

        def add_turned(rows, source, ready, s_pe, s_dve):
            pe.wait(ready)
            for half in range(2):
                pe.wait(*pre_free[half])
                for t in range(TT // 2):
                    for k in range(KT):
                        m = pe.do(lambda e, half=half, t=t, k=k: e.transpose(
                            pre[half][:, t * DIM + k * P:t * DIM + (k + 1) * P],
                            source[:, k, (half * 2 + t) * P:(half * 2 + t + 1) * P], ident[:, :]), s_pe)
                dve.wait(m)
                part = rows[:, half * 2:half * 2 + 2, :].rearrange("p t d -> p (t d)")
                m = dve.do(lambda e, half=half, part=part: e.tensor_tensor(part, part, pre[half][:, :], ALU.add), s_dve)
                pre_free[half] = [m]
            return m

        def finish(b, summed):
            for k in range(KT):
                act.wait(summed, w_out_ready, prepared[GAIN_B])
                m = act.do(lambda e, k=k: e.activation(mixed[:, k, :], sum_ps[k][:, :], ACT.Copy,
                                                       scale=mod[:, GAIN_B, k, b:b + 1]), s_fin_act)
            sums_read[b] = m
            yield
            m = add_turned(x_rows[b % X_RING], mixed, m, s_fin_pe, s_fin_dve)
            sp.wait(m)
            finished[b] = sp.do(lambda e: e.dma_start(out_rows[b], x_rows[b % X_RING][:, :, :]), s_store[b % X_RING], 16)
            if b + X_RING < BATCH:
                sp.wait(finished[b])
                x_loaded[b + X_RING] = load(sp, x_rows[b % X_RING][:, :, :], x_in_rows[b + X_RING], s_x[b % X_RING])

        sums_read = {}
        TOTAL = BATCH * SLOTS
        up_done, down_done, split_done, act_done, routed, silus, gated = {}, {}, {}, {}, {}, {}, {}
        row_loads = {}

        def split_slot(g):
            s = g % SLOTS
            up_raw, down_raw = w_slots[:, s, 0:UP_COLS], w_slots[:, s, UP_COLS:SLOT_COLS]
            act.wait(w_loaded[s])
            marks = []
            for queue, s_lo, dst_hi, dst_lo, raw, freed in (
                    (pool, s_up_lo, up_hi[g % 2], up_lo[g % 2], up_raw, up_done.get(g - 2)),
                    (dve, s_down_lo, down_hi[g % DOWN_RING], down_lo[g % DOWN_RING], down_raw,
                     down_done.get(g - DOWN_RING))):
                if freed:
                    act.wait(freed)
                hi = act.do(lambda e, d=dst_hi, r=raw: e.copy(d[:, :], r), s_split_hi)
                queue.wait(hi)
                marks.append(queue.do(lambda e, d=dst_lo, h=dst_hi, r=raw: e.tensor_tensor(
                    d[:, :], r, h[:, :].bitcast(F32), ALU.subtract), s_lo))
            split_done[g] = marks

        def load_rows(g):
            b, first = g // SLOTS, (g % SLOTS - SHARED_SLOTS) * P
            ring = routed_index(g) % ROUTING_RING
            sp.wait(routing_ready[b])
            before = [x for x in row_loads if row_loads[x][0] == ring]
            if before:
                sp.wait(routed[max(before)])
            at = 0
            while at < P:
                expert = (first + at) // EXPERT_HIDDEN
                to = min(P, (expert + 1) * EXPERT_HIDDEN - first)
                m = sp.do(lambda e, at=at, to=to, x=expert: e.dma_start(
                    routing_rows[ring][at:to, :], routing_dram[b, x:x + 1, :].broadcast_to([to - at, SEQ])),
                    s_rows[ring], 16)
                at = to
            row_loads[g] = (ring, m)

        def routed_index(g):
            return g // SLOTS * ROUTED_SLOTS + g % SLOTS - SHARED_SLOTS

        def is_shared(g):
            return g % SLOTS < SHARED_SLOTS

        def activate(g):
            buf, ring = hidden[g % 3], g % 2
            dve.wait(silus[g] if is_shared(g) else routed[g], up_done[g])
            m = dve.do(lambda e: e.tensor_tensor(buf[:, :], buf[:, :], up_ps[g % 2][:, :], ALU.mult), s_act)
            gated[g] = m
            act.wait(m)
            if g >= 2:
                act.wait(down_done[g - 2])
            hi = act.do(lambda e: e.copy(act_hi[ring][:, :], buf[:, :]), s_act_hi)
            dve.wait(hi)
            act_done[g] = dve.do(lambda e: e.tensor_tensor(
                act_lo[ring][:, :], buf[:, :], act_hi[ring][:, :].bitcast(F32), ALU.subtract), s_act_lo)

        def down(g):
            b, s = divmod(g, SLOTS)
            pe.wait(act_done[g], *split_done[g])
            if s == 0 and b >= 1:
                pe.wait(sums_read[b - 1])
            for k in range(KT):
                hi, lo = (w[g % DOWN_RING][:, k * P:(k + 1) * P] for w in (down_hi, down_lo))
                for n, (a, v) in enumerate(((hi, act_hi), (hi, act_lo), (lo, act_hi))):
                    m = pe.do(lambda e, k=k, a=a, v=v, n=n: e.matmul(
                        sum_ps[k][:, :], a, v[g % 2][:, :], start=s == 0 and n == 0,
                        stop=s == SLOTS - 1 and n == 2), s_down_mm if (k, n) == (KT - 1, 2) else None)
            down_done[g] = m

        def up(g):
            b = g // SLOTS
            pe.wait(*h_ready[b], *split_done[g])
            for name, ps, part, sem_ in (("gate", gate_ps, 0, s_gate_mm), ("up", up_ps, 1, s_up_mm)):
                if g >= 2:
                    pe.wait(gated[g - 2] if name == "up" else silus[g - 2])
                pairs = []
                for k in range(KT):
                    cols = slice((2 * k + part) * P, (2 * k + part + 1) * P)
                    pairs.append(((up_hi[g % 2][:, cols], up_lo[g % 2][:, cols]),
                                  (h_hi[b % 2][:, k, :], h_lo[b % 2][:, k, :])))
                m = split_products(ps[g % 2][:, :], pairs, sem_)
                if name == "gate":
                    gate_done = m
            up_done[g] = m
            if g % SLOTS == SLOTS - 1:
                block_up_done[b] = m
            return gate_done

        for _ in prepare(0): pass
        split_slot(0)
        preparing, finishing = iter(()), iter(())
        for g in range(TOTAL + DOWN_LAG):
            b, s = divmod(g, SLOTS)
            if g + 1 < TOTAL:
                split_slot(g + 1)
            if g < TOTAL:
                upcoming, start = divmod(g + PREPARE_AHEAD, SLOTS)
                if (start == 0 or g == 0) and upcoming + 1 < BATCH:
                    preparing = chain(preparing, prepare(upcoming + 1))
                gate_done = up(g)
                if not is_shared(g):
                    load_rows(g)
                buf = hidden[g % 3]
                act.wait(gate_done)
                m = act.do(lambda e, g=g, buf=buf: e.activation(buf[:, :], gate_ps[g % 2][:, :], ACT.Tanh,
                                                                scale=0.5), s_tanh)
                dve.wait(m)
                silus[g] = dve.do(lambda e, g=g, buf=buf: e.scalar_tensor_tensor(
                    out=buf[:, :], in0=buf[:, :], scalar=1.0, in1=gate_ps[g % 2][:, :],
                    op0=ALU.add, op1=ALU.mult), s_silu)
                if not is_shared(g):
                    ring, rows_in = row_loads[g]
                    pool.wait(silus[g], rows_in)
                    routed[g] = pool.do(lambda e, buf=buf, ring=ring: e.tensor_tensor(
                        buf[:, :], buf[:, :], routing_rows[ring][:, :], ALU.mult), s_routed)
            if 0 <= g - 1 < TOTAL:
                activate(g - 1)
            if g >= DOWN_LAG:
                down(g - DOWN_LAG)
                if (g - DOWN_LAG) % SLOTS == SLOTS - 1:
                    finishing = finish((g - DOWN_LAG) // SLOTS, down_done[g - DOWN_LAG])
            next(finishing, None)
            next(preparing, None)
        for _ in finishing:
            pass
        for b in range(BATCH):
            sp.wait(finished[b])

        block = ctx.enter_context(nc.Block())
        block.sync(sp.play)
        block.tensor(pe.play)
        block.scalar(act.play)
        block.vector(dve.play)
        block.gpsimd(pool.play)


def slot_weights(gate, up, down):
    rows = gate.shape[0]
    slots = -(-rows // P)
    laid = np.zeros((P, slots, SLOT_COLS), gate.dtype)
    for s in range(slots):
        n = min(P, rows - s * P)
        part = slice(s * P, s * P + n)
        for k in range(KT):
            for j, w in enumerate((gate, up)):
                at = (2 * k + j) * P
                laid[:, s, at:at + n] = w[part, k * P:(k + 1) * P].T
        laid[:n, s, UP_COLS:] = down[:, part].T
    return laid


def kernel(**inputs):
    import concourse.bacc as _bacc
    from concourse.bass_utils import run_bass_kernel_spmd as _run

    a = {n.removeprefix("L0_"): np.asarray(v) for n, v in inputs.items()}
    w1, w2 = a["ffn_w1"], a["ffn_w2"]
    shared1, shared2 = a["ffn_shared_w1"], a["ffn_shared_w2"]
    gates = a["attn_W_gate"].reshape(HEADS, 4, HEAD_DIM, DIM)[:, list(REFERENCE_GATES)]
    gate_biases = a["attn_b_gate"].reshape(HEADS, 4, HEAD_DIM)[:, list(REFERENCE_GATES)]
    arrays = {
        "x": a["attn_x"],
        "w_in": a["attn_W_in"],
        "w_gate_t": gates.transpose(3, 1, 0, 2).reshape(DIM, 4 * DIM),
        "b_gate": gate_biases.transpose(1, 0, 2).reshape(4 * KT, P).T,
        "rms_w": a["attn_rms_w"].reshape(HEAD_DIM, 1),
        "w_out_t": a["attn_W_out"].T,
        "router_t": a["ffn_gate_w"].T,
        "shared_w": slot_weights(shared1[:SHARED_HIDDEN], shared1[SHARED_HIDDEN:], shared2),
        "routed_w": slot_weights(w1[:, :EXPERT_HIDDEN].reshape(-1, DIM), w1[:, EXPERT_HIDDEN:].reshape(-1, DIM),
                                 w2.transpose(1, 0, 2).reshape(DIM, -1)),
        "cond_t": a["c"].T,
        "w_mod": a["wmod"],
    }
    arrays = {n: np.ascontiguousarray(v) for n, v in arrays.items()}
    nc = _bacc.Bacc("TRN2", target_bir_lowering=False, num_devices=1)
    args = [nc.dram_tensor(n, v.shape, mybir.dt.from_np(v.dtype), kind="ExternalInput").ap()
            for n, v in arrays.items()]
    args.append(nc.dram_tensor("out", (BATCH, SEQ, DIM), F32, kind="ExternalOutput").ap())
    adaln_program(nc, *args)
    return _run(nc, [arrays], core_ids=[0]).results[0]["out"]
```

```python
from contextlib import ExitStack
from itertools import chain

import numpy as np

import concourse.bass as bass
from concourse import mybir

F32 = mybir.dt.float32
F32R = mybir.dt.float32r
I32 = mybir.dt.int32
ALU = mybir.AluOpType
ACT = mybir.ActivationFunctionType
AX = mybir.AxisListType

P = 128
BATCH, SEQ, DIM = 4, 512, 256
HEADS, HEAD_DIM = 4, 64
EXPERTS, EXPERT_HIDDEN, TOP_K = 16, 176, 6
SHARED_HIDDEN = 352
LN_EPS, RMS_EPS, GATE_FLOOR = 1e-5, 1e-6, 0.25

KT = DIM // P
TT = SEQ // P
GATE_C, GATE_I, GATE_F, GATE_O = range(4)
REFERENCE_GATES = (3, 0, 1, 2)
HEADS_PER_TILE = P // HEAD_DIM
SHARED_SLOTS = -(-SHARED_HIDDEN // P)
ROUTED_SLOTS = EXPERTS * EXPERT_HIDDEN // P
SLOTS = SHARED_SLOTS + ROUTED_SLOTS
UP_COLS = KT * 2 * P
SLOT_COLS = UP_COLS + DIM
SHIFT_A, SCALE_A, GAIN_A, SHIFT_B, SCALE_B, GAIN_B = range(6)
MODS = 6
MAX8 = 8
BIG_PROB = 2.0
RSQRT_SEED = float(0x5F3759DF)
DOWN_LAG = 2
ROUTING_RING = 3
DOWN_RING = 4
X_RING = 3
SECOND_STEPS = {2: 1, 4: 2, 5: 1, 8: 1, 14: 1, 15: 1, 16: 1, 17: 1}
OTHER_MODS_STEPS = (1, 10, 11)
SPLIT_STEP = 11
KEEP_BUSY = {6: 14, 11: 10}
WARM_UP = 12
FINISH_LAGS = (9, 1)
PREPARE_AHEAD = 3
WORK_TILES = 5
STAGING_COLS = KT * (MODS + 4) * DIM
TAIL_TILES = WORK_TILES - 2
STAGING_SLOT = SLOTS - -(-(STAGING_COLS + TAIL_TILES * KT * SEQ) // SLOT_COLS)


class Engine:

    def __init__(self, counts):
        self.steps, self.counts, self.waited, self.between = [], counts, {}, []

    def wait(self, *marks):
        for sem, value in marks:
            if self.waited.get(id(sem), 0) < value:
                self.waited[id(sem)] = value
                self.steps.append(lambda e, s=sem, v=value: e.wait_ge(s, v))

    def do(self, step, sem=None, by=1):
        if sem is None:
            self.steps.append(step)
            mark = None
        else:
            self.counts[id(sem)] = self.counts.get(id(sem), 0) + by
            self.steps.append(lambda e: step(e).then_inc(sem, by))
            mark = (sem, self.counts[id(sem)])
        if self.between:
            self.place_one()
        return mark

    def chain(self, first, steps, sem):
        self.place_all()
        for step in steps:
            self.counts[id(sem)] = self.counts.get(id(sem), 0) + 1
            self.between.append((first, step, sem))
            first = (sem, self.counts[id(sem)])
        return first

    def place_one(self):
        before, step, sem = self.between.pop(0)
        self.wait(before)
        self.steps.append(lambda e: step(e).then_inc(sem, 1))

    def place_all(self):
        while self.between:
            self.place_one()

    def play(self, e):
        for step in self.steps:
            step(e)


def adaln_program(nc, x_in, w_in, w_gate_t, b_gate, rms_w, w_out_t, router_t, shared_w, routed_w,
                  cond_t, w_mod, out):
    ctx = ExitStack()
    with ctx:
        def sb(name, shape, dt=F32):
            return ctx.enter_context(nc.sbuf_tensor(name, shape, dt))

        def sem(name):
            return ctx.enter_context(nc.semaphore(name))

        gain_a_dram = nc.dram_tensor("gain_a_dram", [BATCH, DIM], F32, kind="Internal").ap()
        routing_dram = nc.dram_tensor("routing_dram", [BATCH, EXPERTS, SEQ], F32, kind="Internal").ap()

        ident = sb("ident", [P, P])
        head_mean = sb("head_mean", [P, HEADS_PER_TILE])
        w_slots = sb("w_slots", [P, SLOTS, SLOT_COLS])
        w_gates_hi = sb("w_gates_hi", [P, KT, 4 * DIM], F32R)
        w_gates_lo = sb("w_gates_lo", [P, KT, 4 * DIM], F32R)
        w_out = sb("w_out", [P, KT, DIM])
        gain_a_wide = sb("gain_a_wide", [P, DIM])
        w_out_hi = sb("w_out_hi", [P, KT, DIM], F32R)
        w_out_lo = sb("w_out_lo", [P, KT, DIM], F32R)
        router_w = sb("router_w", [P, KT, EXPERTS])
        gate_bias = sb("gate_bias", [P, 4 * KT])
        half_bias = sb("half_bias", [P, 4 * KT])
        rms_scale = sb("rms_scale", [P, 1])
        cond = sb("cond", [P, KT, BATCH])
        cond_tanh = sb("cond_tanh", [P, KT, BATCH])
        cond_silu = sb("cond_silu", [P, KT, BATCH])
        mod = sb("mod", [P, MODS, KT, BATCH])
        gain_sign = sb("gain_sign", [P, KT, BATCH])
        gain_abs = sb("gain_abs", [P, KT, BATCH])

        x_rows = [sb(f"x_rows{i}", [P, TT, DIM]) for i in range(X_RING)]
        h_hi = [sb(f"h_hi{i}", [P, KT, SEQ], F32R) for i in range(2)]
        h_lo = [sb(f"h_lo{i}", [P, KT, SEQ], F32R) for i in range(2)]
        mixed = sb("mixed", [P, KT, SEQ])
        tail = w_slots[:, STAGING_SLOT:SLOTS, :].rearrange("p s c -> p (s c)")
        w_mod_raw = tail[:, 0:KT * MODS * DIM].rearrange("p (k m) -> p k m", k=KT)
        w_gate_raw = tail[:, KT * MODS * DIM:STAGING_COLS].rearrange("p (k m) -> p k m", k=KT)
        work_tail = tail[:, STAGING_COLS:STAGING_COLS + TAIL_TILES * KT * SEQ].rearrange(
            "p (n k t) -> p n k t", n=TAIL_TILES, k=KT)
        mixed_flat = mixed[:, :, :].rearrange("p k t -> p (k t)")
        w_in_raw = mixed_flat[:, 0:KT * DIM].rearrange("p (k m) -> p k m", k=KT)

        NORMS = KT * TT * HEADS_PER_TILE

        class Scratch:

            def __init__(self, n, work, banks):
                self.gate_c, self.gate_f, self.cell, self.gate_o, self.gate_i = work
                self.h_full = self.cell_out = self.gate_i
                self.normed = self.gate_c.rearrange("p k t -> p (k t)").rearrange("p (t d) -> p t d", d=DIM)
                self.square = self.cell_tanh = self.gate_c
                self.inv_rms_wide = self.gate_f.rearrange("p k t -> p (k t)").rearrange(
                    "p (k t c) -> p k t c", k=KT, c=P)
                self.w_scaled = self.gate_f.rearrange("p k t -> p (k t)")[:, 0:KT * DIM].rearrange(
                    "p (k m) -> p k m", k=KT)
                self.cell_out_hi = sb(f"cell_out_hi{n}", [P, KT, SEQ], F32R)
                self.cell_out_lo = sb(f"cell_out_lo{n}", [P, KT, SEQ], F32R)
                self.stats = sb(f"stats{n}", [P, TT, 6])
                self.mean_var = sb(f"mean_var{n}", [P, TT, 2])
                self.ln = [sb(f"ln_{i}{n}", [P, TT], dt) for i, dt in (("in", F32), ("seed", I32), ("y", I32), ("t", F32))]
                self.rms = [sb(f"rms_{i}{n}", [P, NORMS], dt)
                            for i, dt in (("in", F32), ("seed", I32), ("y", I32), ("t", F32))]
                self.banks = banks
                self.bank_free = [[], []]

        neg_max = sb("neg_max", [P, TT])
        exps = sb("exps", [P, TT, EXPERTS])
        exp_sum = sb("exp_sum", [P, TT])
        exp_inv = sb("exp_inv", [P, TT])
        PADDED = EXPERTS + MAX8 - TOP_K
        probs = sb("probs", [P, TT, PADDED])
        best8 = sb("best8", [P, TT, MAX8])
        taken = sb("taken", [P, TT, PADDED])
        routing = sb("routing", [P, TT, EXPERTS])
        routing_t = sb("routing_t", [EXPERTS, SEQ])

        up_hi = [sb(f"up_hi{i}", [P, UP_COLS], F32R) for i in range(2)]
        up_lo = [sb(f"up_lo{i}", [P, UP_COLS], F32R) for i in range(2)]
        down_hi = [sb(f"down_hi{i}", [P, DIM], F32R) for i in range(DOWN_RING)]
        down_lo = [sb(f"down_lo{i}", [P, DIM], F32R) for i in range(DOWN_RING)]
        hidden = [sb(f"hidden{i}", [P, SEQ]) for i in range(3)]
        act_hi = [sb(f"act_hi{i}", [P, SEQ], F32R) for i in range(2)]
        act_lo = [sb(f"act_lo{i}", [P, SEQ], F32R) for i in range(2)]
        routing_rows = [sb(f"routing_rows{i}", [P, SEQ]) for i in range(ROUTING_RING)]

        def bank(name):
            return ctx.enter_context(nc.psum_tensor(name, [P, SEQ], F32))

        pre = [bank(f"pre{i}") for i in range(2)]
        gate_ps = [bank(f"gate_ps{i}") for i in range(2)]
        up_ps = [bank(f"up_ps{i}") for i in range(2)]
        sum_ps = [bank(f"sum_ps{i}") for i in range(KT)]

        scratch_0 = Scratch(0, [sb(f"work{i}", [P, KT, SEQ])[:, :, :] for i in range(WORK_TILES)], pre)
        scratch_1 = Scratch(1, [work_tail[:, i] for i in range(TAIL_TILES)] + [
            mixed[:, :, :],
            x_rows[2][:, :, :].rearrange("p t d -> p (t d)").rearrange("p (k t) -> p k t", k=KT)], sum_ps)

        counts = {}
        sp, pe, act, dve, pool = (Engine(counts) for _ in range(5))

        s_load = {n: sem(f"s_load_{n}") for n in
                  ("first_mods", "other_mods", "cond", "w_gate_0", "w_gate_1", "w_in", "w_out", "small", "router")}
        s_x = [sem(f"s_x{i}") for i in range(X_RING)]
        after_mods = STAGING_SLOT + STAGING_COLS // SLOT_COLS
        W_PARTS = [(0, 1), (1, 3), (3, 7), (7, STAGING_SLOT), (STAGING_SLOT, after_mods)] + [
                       (s, s + 1) for s in range(after_mods, SLOTS)]
        W_AFTER_MODS, W_AFTER_WORK = 4, 5
        s_w = [sem(f"s_w{i}") for i in range(len(W_PARTS))]
        s_store = [sem(f"s_store{i}") for i in range(X_RING)]
        s_routing_dram = sem("s_routing_dram")
        s_rows = [sem(f"s_rows{i}") for i in range(ROUTING_RING)]
        s_rsqrt, s_setup_chain = sem("s_rsqrt"), sem("s_setup_chain")
        s_gain_dram, s_gain_wide, s_w_out = sem("s_gain_dram"), sem("s_gain_wide"), sem("s_w_out")
        s_const, s_setup_act, s_setup_dve, s_setup_pe = (sem(n) for n in (
            "s_const", "s_setup_act", "s_setup_dve", "s_setup_pe"))
        s_prep_pe, s_prep_act, s_prep_dve, s_prep_pool = (sem(n) for n in (
            "s_prep_pe", "s_prep_act", "s_prep_dve", "s_prep_pool"))
        s_fin_pe, s_fin_act, s_fin_dve = (sem(n) for n in ("s_fin_pe", "s_fin_act", "s_fin_dve"))
        s_gate_mm, s_up_mm, s_down_mm = (sem(n) for n in ("s_gate_mm", "s_up_mm", "s_down_mm"))
        s_split_hi, s_up_lo, s_down_lo = sem("s_split_hi"), sem("s_up_lo"), sem("s_down_lo")
        s_tanh, s_silu, s_routed, s_act, s_act_hi, s_act_lo = (sem(n) for n in (
            "s_tanh", "s_silu", "s_routed", "s_act", "s_act_hi", "s_act_lo"))

        def split_products(dst, pairs, sem_=None):
            last, n = None, 0
            for (a_hi, a_lo), (b_hi, b_lo) in pairs:
                for a, b in ((a_hi, b_hi), (a_hi, b_lo), (a_lo, b_hi)):
                    n += 1
                    first, end = n == 1, n == 3 * len(pairs)
                    last = pe.do(lambda e, a=a, b=b, f=first, l=end: e.matmul(dst, a, b, start=f, stop=l),
                                 sem_ if end else None)
            return last

        def load(queue, dst, src, sem_):
            return queue.do(lambda e: e.dma_start(dst, src), sem_, 16)

        x_in_rows = x_in.rearrange("b (t p) d -> b p t d", p=P)
        out_rows = out.rearrange("b (t p) d -> b p t d", p=P)
        w_mod_rows = w_mod.rearrange("(k p) m -> p k m", p=P)
        w_gate_rows = w_gate_t.rearrange("(k p) m -> p k m", p=P)
        FIRST_MODS = (SCALE_A + 1) * DIM
        cond_in = load(act, cond[:, :, :], cond_t.rearrange("(k p) b -> p k b", p=P), s_load["cond"])
        x_loaded = {0: load(sp, x_rows[0][:, :, :], x_in_rows[0], s_x[0])}
        w_in_in = load(sp, w_in_raw, w_in.rearrange("(k p) m -> p k m", p=P), s_load["w_in"])
        w_gate_in = {0: load(sp, w_gate_raw[:, :, 0:SEQ], w_gate_rows[:, :, 0:SEQ], s_load["w_gate_0"])}
        first_mods_in = load(sp, w_mod_raw[:, :, 0:FIRST_MODS], w_mod_rows[:, :, 0:FIRST_MODS], s_load["first_mods"])
        w_gate_in[1] = load(sp, w_gate_raw[:, :, SEQ:2 * SEQ], w_gate_rows[:, :, SEQ:2 * SEQ], s_load["w_gate_1"])
        load(sp, gate_bias[:, :], b_gate, s_load["small"])
        for h in range(HEADS_PER_TILE):
            small_in = load(sp, rms_scale[h * HEAD_DIM:(h + 1) * HEAD_DIM, :], rms_w, s_load["small"])
        x_loaded[1] = load(sp, x_rows[1][:, :, :], x_in_rows[1], s_x[1])
        other_mods_in = load(sp, w_mod_raw[:, :, FIRST_MODS:], w_mod_rows[:, :, FIRST_MODS:], s_load["other_mods"])
        w_out_in = load(sp, w_out[:, :, :], w_out_t.rearrange("(k p) m -> p k m", p=P), s_load["w_out"])
        router_in = load(sp, router_w[:, :, :], router_t.rearrange("(k p) m -> p k m", p=P), s_load["router"])
        w_loaded = {}

        def load_slots(i):
            a, b = W_PARTS[i]
            src = shared_w[:, a:b, :] if b <= SHARED_SLOTS else routed_w[:, a - SHARED_SLOTS:b - SHARED_SLOTS, :]
            mark = load(sp, w_slots[:, a:b, :], src, s_w[i])
            for s in range(a, b):
                w_loaded[s] = mark

        for i in range(W_AFTER_MODS):
            load_slots(i)

        pool.do(lambda e: e.memset(ident[:, :], 0.0), s_const)
        pool.do(lambda e: e.memset(head_mean[:, :], 0.0), s_const)
        zeroed = pool.do(lambda e: e.memset(probs[:, :, EXPERTS:PADDED], BIG_PROB), s_const)
        pool.wait(zeroed)
        consts_in = pool.do(lambda e: e.affine_select(out=ident[:, :], in_=ident[:, :], compare_op=ALU.not_equal, fill=1.0,
                                          base=0, pattern=[[-1, P]], channel_multiplier=1), s_const)
        for h in range(HEADS_PER_TILE):
            pool.wait(consts_in)
            consts_in = pool.do(lambda e, h=h: e.memset(
                head_mean[h * HEAD_DIM:(h + 1) * HEAD_DIM, h:h + 1], 1.0 / HEAD_DIM), s_const)

        pool.wait(consts_in)
        act.wait(cond_in)
        m = act.do(lambda e: e.activation(cond_tanh[:, :, :], cond[:, :, :], ACT.Tanh, scale=0.5), s_setup_act)
        dve.wait(m)
        silu2 = dve.do(lambda e: e.scalar_tensor_tensor(
            out=cond_silu[:, :, :], in0=cond_tanh[:, :, :], scalar=1.0, in1=cond[:, :, :],
            op0=ALU.add, op1=ALU.mult), s_setup_dve)
        mod_ps = gate_ps[0][:, 0:MODS * KT * BATCH]
        prepared = {}

        def one_plus(i):
            return [lambda e: e.tensor_scalar(mod[:, i], mod[:, i], 1.0, None, ALU.add)]

        def floored_gain(gain, gain_sign, gain_abs):
            return [
                lambda e: e.tensor_scalar(gain_sign, gain, 0.0, 2.0, ALU.is_ge, ALU.mult),
                lambda e: e.tensor_scalar(gain_sign, gain_sign, -1.0, None, ALU.add),
                lambda e: e.tensor_tensor(gain_abs, gain, gain_sign, ALU.mult),
                lambda e: e.tensor_scalar(gain_abs, gain_abs, GATE_FLOOR, 0.5, ALU.max, ALU.mult),
                lambda e: e.tensor_tensor(gain, gain_abs, gain_sign, ALU.mult)]

        def modulation(first, last, steps):
            pe.wait(*prepared.values())
            for n in range(first * KT, last * KT):
                for k in range(KT):
                    m = pe.do(lambda e, n=n, k=k: e.matmul(
                        mod_ps[:, n * BATCH:(n + 1) * BATCH], w_mod_raw[:, k, n * P:(n + 1) * P],
                        cond_silu[:, k, :], start=k == 0, stop=k == KT - 1), s_setup_pe)
            prepared[last - 1] = dve.chain(m, [lambda e: e.tensor_scalar(
                mod[:, first:last], mod_ps[:, first * KT * BATCH:last * KT * BATCH].rearrange(
                    "p (m k b) -> p m k b", m=last - first, k=KT), 0.5, None, ALU.mult)] + steps, s_setup_chain)

        def first_gain():
            pe.wait(*prepared.values())
            rows_ps = gate_ps[0][0:BATCH, DIM:2 * DIM]
            for k in range(KT):
                m = pe.do(lambda e, k=k: e.matmul(
                    rows_ps, cond_silu[:, k, :], w_mod_raw[:, k, GAIN_A * DIM:(GAIN_A + 1) * DIM],
                    start=k == 0, stop=k == KT - 1), s_setup_pe)
            gain_a, signs, sizes = hidden[0][0:BATCH, 0:DIM], hidden[1][0:BATCH, 0:DIM], hidden[2][0:BATCH, 0:DIM]
            prepared[GAIN_A] = dve.chain(m, [lambda e: e.tensor_scalar(
                gain_a, rows_ps, 0.5, None, ALU.mult)] + floored_gain(gain_a, signs, sizes), s_setup_chain)
            sp.wait(prepared[GAIN_A])
            gain_a_stored = sp.do(lambda e: e.dma_start(gain_a_dram, gain_a), s_gain_dram, 16)
            sp.wait(gain_a_stored)

        def widen_gain(b):
            if b >= 1:
                sp.wait(*w_out_scaled[b - 1])
            gain_in[b] = load(sp, gain_a_wide[:, :], gain_a_dram[b:b + 1, :].broadcast_to([P, DIM]), s_gain_wide)

        def scale_w_out(w, b, room_free):
            pool.wait(room_free, gain_in[b], w_out_in)
            scaled = pool.do(lambda e: e.tensor_tensor(
                w.w_scaled, w_out[:, :, :], gain_a_wide[:, :].rearrange("p (o m) -> p o m", o=1).broadcast_to(
                    [P, KT, DIM]), ALU.mult), s_w_out)
            act.wait(scaled)
            if b >= 1:
                act.wait(projected[b - 1])
            hi = act.do(lambda e: e.copy(w_out_hi[:, :, :], w.w_scaled), s_w_out)
            pool.wait(hi)
            lo = pool.do(lambda e: e.tensor_tensor(
                w_out_lo[:, :, :], w.w_scaled, w_out_hi[:, :, :].bitcast(F32), ALU.subtract), s_w_out)
            w_out_scaled[b] = [scaled, lo]

        gain_in, w_out_scaled, projected = {}, {}, {}

        w_gates_ready = {}
        combined_ps = [up_ps[0], up_ps[1]]

        def combine_weights(half):
            pe.wait(w_in_in, w_gate_in[half])
            if half == 1:
                pe.wait(w_gates_ready[0])
            for k in range(KT):
                cols = slice(half * SEQ, (half + 1) * SEQ)
                for kk in range(KT):
                    m = pe.do(lambda e, k=k, kk=kk, cols=cols: e.matmul(
                        combined_ps[k][:, :], w_in_raw[:, kk, k * P:(k + 1) * P], w_gate_raw[:, kk, cols],
                        start=kk == 0, stop=kk == KT - 1), s_setup_pe)
                act.wait(m)
                hi = act.do(lambda e, k=k, cols=cols: e.copy(w_gates_hi[:, k, cols], combined_ps[k][:, :]),
                            s_setup_act)
                dve.wait(hi)
                w_gates_ready[half] = dve.do(lambda e, k=k, cols=cols: e.tensor_tensor(
                    w_gates_lo[:, k, cols], combined_ps[k][:, :], w_gates_hi[:, k, cols].bitcast(F32),
                    ALU.subtract), s_setup_dve)

        def rsqrt(value, ready, seed, y, tmp):
            yf = y.bitcast(F32)
            newton = [
                lambda e: e.tensor_tensor(tmp, value, yf, ALU.mult),
                lambda e: e.scalar_tensor_tensor(out=tmp, in0=tmp, scalar=-0.5, in1=yf, op0=ALU.mult, op1=ALU.mult),
                lambda e: e.scalar_tensor_tensor(out=yf, in0=tmp, scalar=1.5, in1=yf, op0=ALU.add, op1=ALU.mult)]
            return dve.chain(ready, [
                lambda e: e.tensor_scalar(seed, value.bitcast(I32), 1, None, ALU.logical_shift_right),
                lambda e: e.tensor_scalar(y, seed, -1.0, RSQRT_SEED, ALU.mult, ALU.add)] + 3 * newton, s_rsqrt)

        def norm_rows(w, rows, ready):
            stats, mean_var, (ln_in, ln_seed, ln_y, ln_t) = w.stats, w.mean_var, w.ln
            dve.wait(*ready)
            for t in range(TT):
                m = dve.do(lambda e, t=t: e.bn_stats(stats[:, t, :], rows[:, t, :]), s_prep_dve)
            dve.wait(m)
            dve.wait(m)
            for t in range(TT):
                m = dve.do(lambda e, t=t: e.bn_aggr(mean_var[:, t, :], stats[:, t, :]), s_prep_dve)
            dve.wait(m)
            m = dve.do(lambda e: e.tensor_scalar(ln_in[:, :], mean_var[:, :, 1], LN_EPS, None, ALU.add), s_prep_dve)
            m = rsqrt(ln_in[:, :], m, ln_seed[:, :], ln_y[:, :], ln_t[:, :])
            yield
            yield
            dve.place_all()
            dve.wait(m)
            inv = ln_y[:, :].bitcast(F32)
            for t in range(TT):
                m = dve.do(lambda e, t=t: e.tensor_scalar(
                    w.normed[:, t, :], rows[:, t, :], mean_var[:, t, 0:1], inv[:, t:t + 1],
                    ALU.subtract, ALU.mult), s_prep_dve)
            yield
            return m

        def split_rows(hi, lo, full, ready, hi_free):
            dve.wait(ready, *hi_free)
            his = [dve.do(lambda e, k=k: e.tensor_copy(hi[:, k, :], full[:, k, :]), s_prep_dve) for k in range(KT)]
            los = []
            for k, (queue, sem_) in enumerate(((dve, s_prep_dve), (pool, s_prep_pool))):
                queue.wait(his[k])
                los.append(queue.do(lambda e, k=k: e.tensor_tensor(
                    lo[:, k, :], full[:, k, :], hi[:, k, :].bitcast(F32), ALU.subtract), sem_))
            return los

        def turn_and_modulate(w, b, normed_ready, mods_ready, scale, shift, h, h_users):
            pre, pre_free = w.banks, w.bank_free
            pe.wait(normed_ready, consts_in)
            for k in range(KT):
                pe.wait(*pre_free[k])
                for t in range(TT):
                    m = pe.do(lambda e, k=k, t=t: e.transpose(
                        pre[k][:, t * P:(t + 1) * P], w.normed[:, t, k * P:(k + 1) * P], ident[:, :]),
                        s_prep_pe if t == TT - 1 else None)
                act.wait(m, mods_ready)
                full = act.do(lambda e, k=k: e.activation(
                    w.h_full[:, k, :], pre[k][:, :], ACT.Identity, bias=mod[:, shift, k, b:b + 1],
                    scale=mod[:, scale, k, b:b + 1]), s_prep_act)
                pre_free[k] = [full]
            yield
            los = split_rows(h_hi[h], h_lo[h], w.h_full, full, h_users())
            return full, los

        block_up_done = {}
        finished = {}
        h_ready, h_written, router_done = {}, {}, {}
        routing_ready = {}

        def prepare(w, b):
            h_full, gate_i, gate_c, gate_f, gate_o, cell = w.h_full, w.gate_i, w.gate_c, w.gate_f, w.gate_o, w.cell
            square = w.square
            rows, h = x_rows[b % X_RING], b % 2
            h_users = lambda: [block_up_done[b - 2]] if b >= 2 else []
            m = yield from norm_rows(w, rows, [x_loaded[b]])
            full, los = yield from turn_and_modulate(w, b, m, prepared[SCALE_A], SCALE_A, SHIFT_A, h, h_users)

            def gate(p, which, k, dst, func, scale, bias):
                pre, pre_free = w.banks, w.bank_free
                n = which * KT + k
                cols = slice(n * P, (n + 1) * P)
                pe.wait(w_gates_ready[which // 2], *pre_free[p])
                mm = split_products(pre[p][:, :], [
                    ((w_gates_hi[:, kk, cols], w_gates_lo[:, kk, cols]),
                     (h_hi[h][:, kk, :], h_lo[h][:, kk, :])) for kk in range(KT)], s_prep_pe)
                act.wait(mm, bias_ready)
                done = act.do(lambda e: e.activation(dst[:, k, :], pre[p][:, :], func, bias=bias[:, n:n + 1],
                                                     scale=scale), s_prep_act)
                pre_free[p] = [done]
                return mm, done

            def input_gates(k):
                _, c = gate(0, GATE_C, k, gate_c, ACT.Tanh, 1.0, gate_bias)
                _, i = gate(1, GATE_I, k, gate_i, ACT.Exp, 1.0, gate_bias)
                return c, i

            def other_gates(k):
                _, f = gate(0, GATE_F, k, gate_f, ACT.Tanh, 0.5, half_bias)
                mm, o = gate(1, GATE_O, k, gate_o, ACT.Tanh, 0.5, half_bias)
                return mm, f, o

            def gated_input(k, c, i):
                pool.wait(c, i)
                return pool.do(lambda e: e.tensor_tensor(gate_i[:, k, :], gate_i[:, k, :], gate_c[:, k, :],
                                                         ALU.mult), s_prep_pool)

            def recurrence(k, f, gated_in):
                dve.wait(f)
                m = dve.do(lambda e: e.tensor_scalar(gate_f[:, k, :], gate_f[:, k, :], 0.5, 0.5,
                                                     ALU.mult, ALU.add), s_prep_dve)
                dve.wait(m, gated_in)
                m = dve.do(lambda e: e.tensor_tensor_scan(
                    cell[:, k, :], gate_f[:, k, :], gate_i[:, k, :], 0.0, ALU.mult, ALU.add), s_prep_dve)
                act.wait(m)
                return act.do(lambda e: e.activation(square[:, k, :], cell[:, k, :], ACT.Square), s_prep_act)

            def mean_squares(k, squared):
                pre, pre_free = w.banks, w.bank_free
                pe.wait(squared)
                if k == 0:
                    pe.wait(*pre_free[0])
                for t in range(TT):
                    at = (k * TT + t) * HEADS_PER_TILE
                    m = pe.do(lambda e, t=t, at=at: e.matmul(
                        pre[0][:, at:at + HEADS_PER_TILE], square[:, k, t * P:(t + 1) * P], head_mean[:, :],
                        start=True, stop=True), s_prep_pe)
                return m

            yield
            pe.wait(*los)
            if b >= 1:
                widen_gain(b)
            c0, i0 = input_gates(0)
            yield
            gated0 = gated_input(0, c0, i0)
            _, f0, o0 = other_gates(0)
            yield
            squared0 = recurrence(0, f0, gated0)
            c1, i1 = input_gates(1)
            yield
            gated1 = gated_input(1, c1, i1)
            gates_done, f1, o1 = other_gates(1)
            yield
            squared1 = recurrence(1, f1, gated1)
            yield
            mean_squares(0, squared0)
            m = mean_squares(1, squared1)
            dve.wait(m)
            m = dve.do(lambda e, ps=w.banks[0]: e.tensor_scalar(w.rms[0][:, :], ps[:, 0:NORMS], RMS_EPS, None, ALU.add), s_prep_dve)
            w.bank_free[0] = [m]
            m = rsqrt(w.rms[0][:, :], m, *(v[:, :] for v in w.rms[1:]))
            yield
            yield
            dve.place_all()
            dve.wait(m)
            inv = w.rms[2][:, :].bitcast(F32).rearrange("p (n o) -> p n o", o=1)
            wide = w.inv_rms_wide.rearrange("p k t c -> p (k t c)").rearrange("p (n d) -> p n d", d=HEAD_DIM)
            spread = dve.do(lambda e: e.tensor_copy(wide, inv.broadcast_to([P, NORMS, HEAD_DIM])), s_prep_dve)
            yield
            pe.wait(spread)
            scaled = []
            for k in range(KT):
                pe.wait(*w.bank_free[k])
                for t in range(TT):
                    m = pe.do(lambda e, k=k, t=t, ps=w.banks[k]: e.transpose(ps[:, t * P:(t + 1) * P],
                                                              w.inv_rms_wide[:, k, t, :], ident[:, :]), s_prep_pe)
                dve.wait(m)
                m = dve.do(lambda e, k=k, ps=w.banks[k]: e.tensor_tensor(cell[:, k, :], cell[:, k, :], ps[:, :], ALU.mult),
                           s_prep_dve)
                w.bank_free[k] = [m]
                scaled.append(m)
            inv_rms_read = m
            yield
            for k, o in enumerate((o0, o1)):
                act.wait(scaled[k])
                m = act.do(lambda e, k=k: e.activation(w.cell_tanh[:, k, :], cell[:, k, :], ACT.Tanh,
                                                       scale=rms_scale[:, 0:1]), s_prep_act)
                dve.wait(m, o)
                m = dve.do(lambda e, k=k: e.scalar_tensor_tensor(
                    out=w.cell_out[:, k, :], in0=gate_o[:, k, :], scalar=1.0, in1=w.cell_tanh[:, k, :],
                    op0=ALU.add, op1=ALU.mult), s_prep_dve)
            scale_w_out(w, b, inv_rms_read)
            yield
            los = split_rows(w.cell_out_hi, w.cell_out_lo, w.cell_out, m, [])
            yield
            pe.wait(*w_out_scaled[b], *los)
            for half in range(2):
                ps = w.banks[half]
                pe.wait(*w.bank_free[half])
                for t in range(TT // 2):
                    at = slice((half * 2 + t) * P, (half * 2 + t + 1) * P)
                    m = split_products(ps[:, t * DIM:(t + 1) * DIM], [
                        ((w.cell_out_hi[:, kk, at], w.cell_out_lo[:, kk, at]),
                         (w_out_hi[:, kk, :], w_out_lo[:, kk, :])) for kk in range(KT)], s_prep_pe)
                projected[b] = m
                dve.wait(m)
                part = rows[:, half * 2:half * 2 + 2, :].rearrange("p t d -> p (t d)")
                m = dve.do(lambda e, part=part, ps=ps: e.tensor_tensor(part, part, ps[:, :], ALU.add), s_prep_dve)
                w.bank_free[half] = [m]
            yield
            m = yield from norm_rows(w, rows, [m])
            full, los = yield from turn_and_modulate(w, b, m, prepared[SCALE_B], SCALE_B, SHIFT_B, h, lambda: [gates_done])
            h_ready[b], h_written[b] = los, full
            yield

        def route(w, b):
            pre, pre_free = scratch_0.banks, scratch_0.bank_free
            pe.wait(h_written[b], router_in, *pre_free[0])
            for t in range(TT):
                for k in range(KT):
                    m = pe.do(lambda e, t=t, k=k: e.matmul(
                        pre[0][:, t * EXPERTS:(t + 1) * EXPERTS], w.h_full[:, k, t * P:(t + 1) * P], router_w[:, k, :],
                        start=k == 0, stop=k == KT - 1), s_prep_pe)
            logits = pre[0][:, 0:TT * EXPERTS].rearrange("p (t x) -> p t x", x=EXPERTS)
            by_expert = lambda v: v.rearrange("p (t o) -> p t o", o=1).broadcast_to([P, TT, EXPERTS])
            router_done[b] = m
            dve.wait(m)
            m = dve.do(lambda e: e.tensor_reduce(neg_max[:, :], logits, AX.X, ALU.max, negate=True), s_prep_dve)
            dve.wait(m)
            m = dve.do(lambda e: e.tensor_tensor(exps[:, :, :], logits, by_expert(neg_max[:, :]), ALU.add), s_prep_dve)
            pre_free[0] = [m]
            act.wait(m)
            m = act.do(lambda e: e.activation(exps[:, :, :], exps[:, :, :], ACT.Exp), s_prep_act)
            yield
            dve.wait(m)
            m = dve.do(lambda e: e.tensor_reduce(exp_sum[:, :], exps[:, :, :], AX.X, ALU.add), s_prep_dve)
            dve.wait(m)
            m = dve.do(lambda e: e.reciprocal(exp_inv[:, :], exp_sum[:, :]), s_prep_dve)
            dve.wait(m)
            m = dve.do(lambda e: e.tensor_tensor(probs[:, :, 0:EXPERTS], exps[:, :, :], by_expert(exp_inv[:, :]),
                                                 ALU.mult), s_prep_dve)
            dve.wait(m, consts_in)
            for t in range(TT):
                m = dve.do(lambda e, t=t: e.max(best8[:, t, :], probs[:, t, :]), s_prep_dve)
            dve.wait(m)
            yield
            for t in range(TT):
                m = dve.do(lambda e, t=t: e.match_replace(taken[:, t, :], best8[:, t, :], probs[:, t, :], -1.0),
                           s_prep_dve)
            dve.wait(m)
            m = dve.do(lambda e: e.scalar_tensor_tensor(
                out=routing[:, :, :], in0=taken[:, :, 0:EXPERTS], scalar=0.0, in1=probs[:, :, 0:EXPERTS],
                op0=ALU.is_lt, op1=ALU.mult), s_prep_dve)
            yield
            pe.wait(m, *pre_free[1])
            for t in range(TT):
                m = pe.do(lambda e, t=t: e.transpose(pre[1][0:EXPERTS, t * P:(t + 1) * P], routing[:, t, :],
                                                     ident[:, :]), s_prep_pe)
            dve.wait(m)
            if b >= 1:
                dve.wait(routing_ready[b - 1])
            m = dve.do(lambda e: e.tensor_copy(routing_t[:, :], pre[1][0:EXPERTS, :]), s_prep_dve)
            pre_free[1] = [m]
            sp.wait(m)
            routing_ready[b] = sp.do(lambda e: e.dma_start(routing_dram[b], routing_t[:, :]), s_routing_dram, 16)

        def add_turned(rows, source, ready, half):
            ps, bank_free = scratch_0.banks[half], scratch_0.bank_free
            pe.wait(*ready, *bank_free[half])
            for t in range(TT // 2):
                for k in range(KT):
                    m = pe.do(lambda e, t=t, k=k: e.transpose(
                        ps[:, t * DIM + k * P:t * DIM + (k + 1) * P],
                        source[:, k, (half * 2 + t) * P:(half * 2 + t + 1) * P], ident[:, :]), s_fin_pe)
            dve.wait(m)
            part = rows[:, half * 2:half * 2 + 2, :].rearrange("p t d -> p (t d)")
            m = dve.do(lambda e: e.tensor_tensor(part, part, ps[:, :], ALU.add), s_fin_dve)
            bank_free[half] = [m]
            return m

        def finish(b, summed):
            last = b == BATCH - 1
            ready = []
            for k in range(KT):
                gain = mod[:, GAIN_B, k, b:b + 1]
                if last and k == KT - 1:
                    dve.wait(summed[k])
                    ready.append(dve.do(lambda e, k=k, gain=gain: e.tensor_scalar(
                        mixed[:, k, :], sum_ps[k][:, :], gain, None, ALU.mult), s_fin_dve))
                else:
                    act.wait(summed[k])
                    ready.append(act.do(lambda e, k=k, gain=gain: e.activation(
                        mixed[:, k, :], sum_ps[k][:, :], ACT.Copy, scale=gain), s_fin_act))
            sums_read[b] = ready
            yield
            rows = x_rows[b % X_RING]
            for half in range(2):
                for _ in range(0 if last else FINISH_LAGS[half]):
                    yield
                sp.wait(add_turned(rows, mixed, ready, half))
                tokens = slice(half * TT // 2, (half + 1) * TT // 2)
                finished[b] = sp.do(lambda e, tokens=tokens: e.dma_start(
                    out_rows[b][:, tokens], rows[:, tokens, :]), s_store[b % X_RING], 16)
            if b + X_RING < BATCH:
                sp.wait(finished[b])
                x_loaded[b + X_RING] = load(sp, rows[:, :, :], x_in_rows[b + X_RING], s_x[b % X_RING])

        sums_read = {}
        TOTAL = BATCH * SLOTS
        up_done, down_done, split_done, act_done, routed, silus, gated = {}, {}, {}, {}, {}, {}, {}
        row_loads, sums_done = {}, {}

        def slot_of(g):
            b, s = divmod(g, SLOTS)
            return s if b < BATCH - 1 or s < SHARED_SLOTS - 1 else SHARED_SLOTS - 1 if s == SLOTS - 1 else s + 1

        def split_slot(g):
            s = slot_of(g)
            up_raw, down_raw = w_slots[:, s, 0:UP_COLS], w_slots[:, s, UP_COLS:SLOT_COLS]
            act.wait(w_loaded[s])
            marks = []
            for queue, s_lo, dst_hi, dst_lo, raw, freed in (
                    (pool, s_up_lo, up_hi[g % 2], up_lo[g % 2], up_raw, up_done.get(g - 2)),
                    (dve, s_down_lo, down_hi[g % DOWN_RING], down_lo[g % DOWN_RING], down_raw,
                     down_done.get(g - DOWN_RING))):
                if freed:
                    act.wait(freed)
                hi = act.do(lambda e, d=dst_hi, r=raw: e.copy(d[:, :], r), s_split_hi)
                queue.wait(hi)
                marks.append(queue.do(lambda e, d=dst_lo, h=dst_hi, r=raw: e.tensor_tensor(
                    d[:, :], r, h[:, :].bitcast(F32), ALU.subtract), s_lo))
            split_done[g] = marks

        def load_rows(g):
            b, first = g // SLOTS, (slot_of(g) - SHARED_SLOTS) * P
            ring = routed_index(g) % ROUTING_RING
            sp.wait(routing_ready[b])
            before = [x for x in row_loads if row_loads[x][0] == ring]
            if before:
                sp.wait(routed[max(before)])
            at = 0
            while at < P:
                expert = (first + at) // EXPERT_HIDDEN
                to = min(P, (expert + 1) * EXPERT_HIDDEN - first)
                m = sp.do(lambda e, at=at, to=to, x=expert: e.dma_start(
                    routing_rows[ring][at:to, :], routing_dram[b, x:x + 1, :].broadcast_to([to - at, SEQ])),
                    s_rows[ring], 16)
                at = to
            row_loads[g] = (ring, m)

        def routed_index(g):
            return g // SLOTS * ROUTED_SLOTS + slot_of(g) - SHARED_SLOTS

        def is_shared(g):
            return slot_of(g) < SHARED_SLOTS

        def activate(g):
            buf, ring = hidden[g % 3], g % 2
            dve.wait(silus[g] if is_shared(g) else routed[g], up_done[g])
            m = dve.do(lambda e: e.tensor_tensor(buf[:, :], buf[:, :], up_ps[g % 2][:, :], ALU.mult), s_act)
            gated[g] = m
            act.wait(m)
            if g >= 2:
                act.wait(down_done[g - 2])
            hi = act.do(lambda e: e.copy(act_hi[ring][:, :], buf[:, :]), s_act_hi)
            dve.wait(hi)
            act_done[g] = dve.do(lambda e: e.tensor_tensor(
                act_lo[ring][:, :], buf[:, :], act_hi[ring][:, :].bitcast(F32), ALU.subtract), s_act_lo)

        def down(g):
            b, s = divmod(g, SLOTS)
            pe.wait(act_done[g], *split_done[g])
            if s == 0:
                pe.wait(*sums_read[b - 1])
            for k in range(KT):
                hi, lo = (w[g % DOWN_RING][:, k * P:(k + 1) * P] for w in (down_hi, down_lo))
                for n, (a, v) in enumerate(((hi, act_hi), (hi, act_lo), (lo, act_hi))):
                    m = pe.do(lambda e, k=k, a=a, v=v, n=n: e.matmul(
                        sum_ps[k][:, :], a, v[g % 2][:, :], start=s == 0 and n == 0,
                        stop=s == SLOTS - 1 and n == 2), s_down_mm if n == 2 else None)
                sums_done[k] = m
            down_done[g] = m

        def up(g):
            b = g // SLOTS
            pe.wait(*h_ready[b], *split_done[g])
            for name, ps, part, sem_ in (("gate", gate_ps, 0, s_gate_mm), ("up", up_ps, 1, s_up_mm)):
                if g >= 2:
                    pe.wait(gated[g - 2] if name == "up" else silus[g - 2])
                pairs = []
                for k in range(KT):
                    cols = slice((2 * k + part) * P, (2 * k + part + 1) * P)
                    pairs.append(((up_hi[g % 2][:, cols], up_lo[g % 2][:, cols]),
                                  (h_hi[b % 2][:, k, :], h_lo[b % 2][:, k, :])))
                m = split_products(ps[g % 2][:, :], pairs, sem_)
                if name == "gate":
                    gate_done = m
            up_done[g] = m
            if g % SLOTS == SLOTS - 1:
                block_up_done[b] = m
            return gate_done

        first, second = prepare(scratch_0, 0), prepare(scratch_1, 1)
        for _ in range(3):
            next(first)
        def keep_busy(n):
            for _ in range(n):
                pe.do(lambda e: e.matmul(gate_ps[1][:, 0:P], ident[:, :], ident[:, :], start=True, stop=True))

        pe.wait(consts_in)
        keep_busy(WARM_UP)
        combine_weights(0)
        pe.wait(silu2, first_mods_in)
        modulation(SHIFT_A, SCALE_A + 1, one_plus(SCALE_A))
        dve.place_all()
        next(first)
        next(first)
        combine_weights(1)
        dve.wait(small_in)
        bias_ready = dve.do(lambda e: e.tensor_scalar(half_bias[:, :], gate_bias[:, :], 0.5, None, ALU.mult),
                            s_setup_dve)
        def gain_b_steps():
            return floored_gain(mod[:, GAIN_B], gain_sign[:, :, :], gain_abs[:, :, :])

        other_mods = [first_gain, lambda: modulation(SHIFT_B, SCALE_B + 1, one_plus(SCALE_B)),
                      lambda: modulation(GAIN_B, MODS, gain_b_steps())]
        pe.wait(other_mods_in)
        step = 0
        while 0 not in h_ready:
            next(first)
            step += 1
            keep_busy(KEEP_BUSY.get(step, 0))
            if step == SPLIT_STEP:
                split_slot(0)
                split_slot(1)
            for _ in range(OTHER_MODS_STEPS.count(step)):
                other_mods.pop(0)()
                if len(other_mods) == 2:
                    widen_gain(0)
                if not other_mods:
                    sp.wait(prepared[GAIN_B])
                    load_slots(W_AFTER_MODS)
            for _ in range(SECOND_STEPS.get(step, 0)):
                next(second)
        pe.wait(prepared[GAIN_B])
        sums_read[-1] = scratch_1.bank_free[0] + scratch_1.bank_free[1]
        scratch_1.banks, scratch_1.bank_free = scratch_0.banks, scratch_0.bank_free
        last_parts = list(range(W_AFTER_WORK, len(W_PARTS)))
        route_first = route(scratch_0, 0)
        preparing, finishing = chain(second, route(scratch_1, 1)), iter(())
        for g in range(TOTAL + DOWN_LAG):
            b, s = divmod(g, SLOTS)
            if 2 <= g + 1 < TOTAL:
                split_slot(g + 1)
            if g < TOTAL:
                upcoming, start = divmod(g + PREPARE_AHEAD, SLOTS)
                if start == 0 and upcoming + 1 < BATCH:
                    preparing = chain(preparing, prepare(scratch_0, upcoming + 1), route(scratch_0, upcoming + 1))
                gate_done = up(g)
                if not is_shared(g):
                    load_rows(g)
                buf = hidden[g % 3]
                act.wait(gate_done)
                m = act.do(lambda e, g=g, buf=buf: e.activation(buf[:, :], gate_ps[g % 2][:, :], ACT.Tanh,
                                                                scale=0.5), s_tanh)
                if g == TOTAL - 1:
                    activate(g - 1)
                dve.wait(m)
                silus[g] = dve.do(lambda e, g=g, buf=buf: e.scalar_tensor_tensor(
                    out=buf[:, :], in0=buf[:, :], scalar=1.0, in1=gate_ps[g % 2][:, :],
                    op0=ALU.add, op1=ALU.mult), s_silu)
                if not is_shared(g):
                    ring, rows_in = row_loads[g]
                    pool.wait(silus[g], rows_in)
                    routed[g] = pool.do(lambda e, buf=buf, ring=ring: e.tensor_tensor(
                        buf[:, :], buf[:, :], routing_rows[ring][:, :], ALU.mult), s_routed)
            if 0 <= g - 1 < TOTAL and g != TOTAL - 1:
                activate(g - 1)
            if g >= DOWN_LAG:
                down(g - DOWN_LAG)
                if (g - DOWN_LAG) % SLOTS == SLOTS - 1:
                    finishing = finish((g - DOWN_LAG) // SLOTS, dict(sums_done))
            next(finishing, None)
            next(preparing, None)
            next(route_first, None)
            if g == 0:
                next(route_first)
            if 1 in h_ready and last_parts:
                sp.wait(*h_ready[1])
                load_slots(last_parts.pop(0))
            if 1 in router_done and 2 not in x_loaded:
                sp.wait(router_done[1])
                x_loaded[2] = load(sp, x_rows[2][:, :, :], x_in_rows[2], s_x[2])
        for _ in finishing:
            pass
        for b in range(BATCH):
            sp.wait(finished[b])

        block = ctx.enter_context(nc.Block())
        block.sync(sp.play)
        block.tensor(pe.play)
        block.scalar(act.play)
        block.vector(dve.play)
        block.gpsimd(pool.play)


def slot_weights(gate, up, down):
    rows = gate.shape[0]
    slots = -(-rows // P)
    laid = np.zeros((P, slots, SLOT_COLS), gate.dtype)
    for s in range(slots):
        n = min(P, rows - s * P)
        part = slice(s * P, s * P + n)
        for k in range(KT):
            for j, w in enumerate((gate, up)):
                at = (2 * k + j) * P
                laid[:, s, at:at + n] = w[part, k * P:(k + 1) * P].T
        laid[:n, s, UP_COLS:] = down[:, part].T
    return laid


def kernel(**inputs):
    import concourse.bacc as _bacc
    from concourse.bass_utils import run_bass_kernel_spmd as _run

    a = {n.removeprefix("L0_"): np.asarray(v) for n, v in inputs.items()}
    w1, w2 = a["ffn_w1"], a["ffn_w2"]
    shared1, shared2 = a["ffn_shared_w1"], a["ffn_shared_w2"]
    gates = a["attn_W_gate"].reshape(HEADS, 4, HEAD_DIM, DIM)[:, list(REFERENCE_GATES)]
    gate_biases = a["attn_b_gate"].reshape(HEADS, 4, HEAD_DIM)[:, list(REFERENCE_GATES)]
    arrays = {
        "x": a["attn_x"],
        "w_in": a["attn_W_in"],
        "w_gate_t": gates.transpose(3, 1, 0, 2).reshape(DIM, 4 * DIM),
        "b_gate": gate_biases.transpose(1, 0, 2).reshape(4 * KT, P).T,
        "rms_w": a["attn_rms_w"].reshape(HEAD_DIM, 1),
        "w_out_t": a["attn_W_out"].T,
        "router_t": a["ffn_gate_w"].T,
        "shared_w": slot_weights(shared1[:SHARED_HIDDEN], shared1[SHARED_HIDDEN:], shared2),
        "routed_w": slot_weights(w1[:, :EXPERT_HIDDEN].reshape(-1, DIM), w1[:, EXPERT_HIDDEN:].reshape(-1, DIM),
                                 w2.transpose(1, 0, 2).reshape(DIM, -1)),
        "cond_t": a["c"].T,
        "w_mod": a["wmod"],
    }
    arrays = {n: np.ascontiguousarray(v) for n, v in arrays.items()}
    nc = _bacc.Bacc("TRN2", target_bir_lowering=False, num_devices=1)
    args = [nc.dram_tensor(n, v.shape, mybir.dt.from_np(v.dtype), kind="ExternalInput").ap()
            for n, v in arrays.items()]
    args.append(nc.dram_tensor("out", (BATCH, SEQ, DIM), F32, kind="ExternalOutput").ap())
    adaln_program(nc, *args)
    return _run(nc, [arrays], core_ids=[0]).results[0]["out"]
```
